# Optimizing a Trainium2 kernel written in Bass

```python
import numpy as np
import jax
import jax.numpy as jnp

def _softmax(x, axis=-1):
    return jax.nn.softmax(x, axis=axis)

def _gelu(x):
    return jax.nn.gelu(x, approximate=True)

def _silu(x):
    return jax.nn.silu(x)

def _sigmoid(x):
    return jax.nn.sigmoid(x)

def _layernorm(x, axis=-1, eps=1e-05):
    m = jnp.mean(x, axis=axis, keepdims=True)
    v = jnp.var(x, axis=axis, keepdims=True)
    return (x - m) / jnp.sqrt(v + eps)

def _scatter_add(tgt, idx, src, axis=0):
    return tgt.at[idx].add(src)

def _segment_sum(src, seg, n):
    return jax.ops.segment_sum(src, seg, n)
kernel_name = 'mk_dlrm_tower_d1_rec_r8_466c62'

def setup_inputs(seed: int=0):
    np.random.seed(seed)
    _w = jnp.asarray

    def _rec_inputs():
        import jax
        import jax.numpy as jnp
        _tk = jax.random.key(seed)
        dense_ctx = jax.random.normal(jax.random.fold_in(_tk, 190), (512, 16), jnp.float32)
        ids = jnp.stack([jax.random.randint(jax.random.fold_in(_tk, 200 + f), (512,), 0, v, jnp.int32) for f, v in enumerate([125000, 125000, 125000, 1000, 12500, 12500, 1250, 12500, 1250, 1000, 1000, 1000, 12500, 1250, 1250, 1250, 1000, 12500, 12500, 12500, 1250, 1250, 1250, 1250, 1000, 1250, 1250, 1000, 1000, 1250, 1250, 1250])], axis=1)
        tbl_0 = 0.05 * jax.random.normal(jax.random.fold_in(_tk, 500 + 0), (125000, 64), jnp.float32)
        tbl_1 = 0.05 * jax.random.normal(jax.random.fold_in(_tk, 500 + 1), (125000, 64), jnp.float32)
        tbl_2 = 0.05 * jax.random.normal(jax.random.fold_in(_tk, 500 + 2), (125000, 64), jnp.float32)
        tbl_3 = 0.05 * jax.random.normal(jax.random.fold_in(_tk, 500 + 3), (1000, 64), jnp.float32)
        tbl_4 = 0.05 * jax.random.normal(jax.random.fold_in(_tk, 500 + 4), (12500, 64), jnp.float32)
        tbl_5 = 0.05 * jax.random.normal(jax.random.fold_in(_tk, 500 + 5), (12500, 64), jnp.float32)
        tbl_6 = 0.05 * jax.random.normal(jax.random.fold_in(_tk, 500 + 6), (1250, 64), jnp.float32)
        tbl_7 = 0.05 * jax.random.normal(jax.random.fold_in(_tk, 500 + 7), (12500, 64), jnp.float32)
        tbl_8 = 0.05 * jax.random.normal(jax.random.fold_in(_tk, 500 + 8), (1250, 64), jnp.float32)
        tbl_9 = 0.05 * jax.random.normal(jax.random.fold_in(_tk, 500 + 9), (1000, 64), jnp.float32)
        tbl_10 = 0.05 * jax.random.normal(jax.random.fold_in(_tk, 500 + 10), (1000, 64), jnp.float32)
        tbl_11 = 0.05 * jax.random.normal(jax.random.fold_in(_tk, 500 + 11), (1000, 64), jnp.float32)
        tbl_12 = 0.05 * jax.random.normal(jax.random.fold_in(_tk, 500 + 12), (12500, 64), jnp.float32)
        tbl_13 = 0.05 * jax.random.normal(jax.random.fold_in(_tk, 500 + 13), (1250, 64), jnp.float32)
        tbl_14 = 0.05 * jax.random.normal(jax.random.fold_in(_tk, 500 + 14), (1250, 64), jnp.float32)
        tbl_15 = 0.05 * jax.random.normal(jax.random.fold_in(_tk, 500 + 15), (1250, 64), jnp.float32)
        tbl_16 = 0.05 * jax.random.normal(jax.random.fold_in(_tk, 500 + 16), (1000, 64), jnp.float32)
        tbl_17 = 0.05 * jax.random.normal(jax.random.fold_in(_tk, 500 + 17), (12500, 64), jnp.float32)
        tbl_18 = 0.05 * jax.random.normal(jax.random.fold_in(_tk, 500 + 18), (12500, 64), jnp.float32)
        tbl_19 = 0.05 * jax.random.normal(jax.random.fold_in(_tk, 500 + 19), (12500, 64), jnp.float32)
        tbl_20 = 0.05 * jax.random.normal(jax.random.fold_in(_tk, 500 + 20), (1250, 64), jnp.float32)
        tbl_21 = 0.05 * jax.random.normal(jax.random.fold_in(_tk, 500 + 21), (1250, 64), jnp.float32)
        tbl_22 = 0.05 * jax.random.normal(jax.random.fold_in(_tk, 500 + 22), (1250, 64), jnp.float32)
        tbl_23 = 0.05 * jax.random.normal(jax.random.fold_in(_tk, 500 + 23), (1250, 64), jnp.float32)
        tbl_24 = 0.05 * jax.random.normal(jax.random.fold_in(_tk, 500 + 24), (1000, 64), jnp.float32)
        tbl_25 = 0.05 * jax.random.normal(jax.random.fold_in(_tk, 500 + 25), (1250, 64), jnp.float32)
        tbl_26 = 0.05 * jax.random.normal(jax.random.fold_in(_tk, 500 + 26), (1250, 64), jnp.float32)
        tbl_27 = 0.05 * jax.random.normal(jax.random.fold_in(_tk, 500 + 27), (1000, 64), jnp.float32)
        tbl_28 = 0.05 * jax.random.normal(jax.random.fold_in(_tk, 500 + 28), (1000, 64), jnp.float32)
        tbl_29 = 0.05 * jax.random.normal(jax.random.fold_in(_tk, 500 + 29), (1250, 64), jnp.float32)
        tbl_30 = 0.05 * jax.random.normal(jax.random.fold_in(_tk, 500 + 30), (1250, 64), jnp.float32)
        tbl_31 = 0.05 * jax.random.normal(jax.random.fold_in(_tk, 500 + 31), (1250, 64), jnp.float32)
        _rk = jax.random.fold_in(_tk, 7)
        W_top1 = 0.0693375 * jax.random.normal(jax.random.fold_in(_tk, 801), (208, 512), jnp.float32)
        W_top2 = 0.0441942 * jax.random.normal(jax.random.fold_in(_tk, 802), (512, 256), jnp.float32)
        W_top3 = 0.0625 * jax.random.normal(jax.random.fold_in(_tk, 803), (256, 1), jnp.float32)
        b_top1 = jnp.zeros((512,), jnp.float32)
        b_top2 = jnp.zeros((256,), jnp.float32)
        return (dense_ctx, ids, tbl_0, tbl_1, tbl_2, tbl_3, tbl_4, tbl_5, tbl_6, tbl_7, tbl_8, tbl_9, tbl_10, tbl_11, tbl_12, tbl_13, tbl_14, tbl_15, tbl_16, tbl_17, tbl_18, tbl_19, tbl_20, tbl_21, tbl_22, tbl_23, tbl_24, tbl_25, tbl_26, tbl_27, tbl_28, tbl_29, tbl_30, tbl_31, W_top1, b_top1, W_top2, b_top2, W_top3)
    dense_ctx, ids, tbl_0, tbl_1, tbl_2, tbl_3, tbl_4, tbl_5, tbl_6, tbl_7, tbl_8, tbl_9, tbl_10, tbl_11, tbl_12, tbl_13, tbl_14, tbl_15, tbl_16, tbl_17, tbl_18, tbl_19, tbl_20, tbl_21, tbl_22, tbl_23, tbl_24, tbl_25, tbl_26, tbl_27, tbl_28, tbl_29, tbl_30, tbl_31, W_top1, b_top1, W_top2, b_top2, W_top3 = _rec_inputs()

    def _L0_rec_setup():
        import jax, jax.numpy as jnp
        import numpy as np
        FIELD = 32
        DIM = 64
        LAYER_SIZE = (128, 128)

        def _cin(x, weights, biases):
            B, F, D = x.shape
            hidden = x
            finals = []
            n_layers = len(weights)
            for i, (w, b) in enumerate(zip(weights, biases)):
                size = w.shape[0]
                z = jnp.einsum('bhd,bfd->bhfd', hidden, x).reshape(B, hidden.shape[1] * F, D)
                y = jnp.einsum('bcd,oc->bod', z, w) + b[None, :, None]
                y = jax.nn.relu(y)
                if i != n_layers - 1:
                    hidden, direct = (y[:, :size // 2, :], y[:, size // 2:, :])
                else:
                    direct = y
                finals.append(direct)
            return jnp.concatenate(finals, axis=1).sum(-1)
        key = jax.random.key(seed)
        ks = jax.random.split(key, 5)
        B = 512
        x = jax.random.normal(ks[0], (B, FIELD, DIM), dtype=jnp.float32)
        field_nums = [FIELD]
        params = {}
        for i, size in enumerate(LAYER_SIZE):
            in_ch = field_nums[-1] * field_nums[0]
            fan = 1.0 / np.sqrt(in_ch)
            params[f'w{i}'] = jax.random.uniform(ks[1 + 2 * i % 4], (size, in_ch), minval=-fan, maxval=fan, dtype=jnp.float32)
            params[f'b{i}'] = jax.random.uniform(ks[2 + 2 * i % 4], (size,), minval=-fan, maxval=fan, dtype=jnp.float32)
            field_nums.append(size // 2)
        return {'cin_inputs': x, 'w0': params['w0'], 'b0': params['b0'], 'w1': params['w1'], 'b1': params['b1']}
    _L0_rec_all = _L0_rec_setup()
    _L0_rec_in = {k: v for k, v in _L0_rec_all.items() if k in ('w0', 'b0', 'w1', 'b1')}
    del _L0_rec_all
    return {'dense_ctx': dense_ctx, 'ids': ids, 'tbl_0': tbl_0, 'tbl_1': tbl_1, 'tbl_2': tbl_2, 'tbl_3': tbl_3, 'tbl_4': tbl_4, 'tbl_5': tbl_5, 'tbl_6': tbl_6, 'tbl_7': tbl_7, 'tbl_8': tbl_8, 'tbl_9': tbl_9, 'tbl_10': tbl_10, 'tbl_11': tbl_11, 'tbl_12': tbl_12, 'tbl_13': tbl_13, 'tbl_14': tbl_14, 'tbl_15': tbl_15, 'tbl_16': tbl_16, 'tbl_17': tbl_17, 'tbl_18': tbl_18, 'tbl_19': tbl_19, 'tbl_20': tbl_20, 'tbl_21': tbl_21, 'tbl_22': tbl_22, 'tbl_23': tbl_23, 'tbl_24': tbl_24, 'tbl_25': tbl_25, 'tbl_26': tbl_26, 'tbl_27': tbl_27, 'tbl_28': tbl_28, 'tbl_29': tbl_29, 'tbl_30': tbl_30, 'tbl_31': tbl_31, 'W_top1': W_top1, 'b_top1': b_top1, 'W_top2': W_top2, 'b_top2': b_top2, 'W_top3': W_top3, 'L0_rec_w0': _L0_rec_in['w0'], 'L0_rec_b0': _L0_rec_in['b0'], 'L0_rec_w1': _L0_rec_in['w1'], 'L0_rec_b1': _L0_rec_in['b1']}

def reference(dense_ctx, ids, tbl_0, tbl_1, tbl_2, tbl_3, tbl_4, tbl_5, tbl_6, tbl_7, tbl_8, tbl_9, tbl_10, tbl_11, tbl_12, tbl_13, tbl_14, tbl_15, tbl_16, tbl_17, tbl_18, tbl_19, tbl_20, tbl_21, tbl_22, tbl_23, tbl_24, tbl_25, tbl_26, tbl_27, tbl_28, tbl_29, tbl_30, tbl_31, W_top1, b_top1, W_top2, b_top2, W_top3, L0_rec_w0, L0_rec_b0, L0_rec_w1, L0_rec_b1):
    import jax
    import jax.numpy as jnp

    def _L0_rec_ref(cin_inputs, w0, b0, w1, b1):
        import jax, jax.numpy as jnp
        import numpy as np
        FIELD = 32
        DIM = 64
        LAYER_SIZE = (128, 128)

        def _cin(x, weights, biases):
            B, F, D = x.shape
            hidden = x
            finals = []
            n_layers = len(weights)
            for i, (w, b) in enumerate(zip(weights, biases)):
                size = w.shape[0]
                z = jnp.einsum('bhd,bfd->bhfd', hidden, x).reshape(B, hidden.shape[1] * F, D)
                y = jnp.einsum('bcd,oc->bod', z, w) + b[None, :, None]
                y = jax.nn.relu(y)
                if i != n_layers - 1:
                    hidden, direct = (y[:, :size // 2, :], y[:, size // 2:, :])
                else:
                    direct = y
                finals.append(direct)
            return jnp.concatenate(finals, axis=1).sum(-1)
        return _cin(cin_inputs, [w0, w1], [b0, b1])
    e = jnp.stack([tbl_0[ids[:, 0]], tbl_1[ids[:, 1]], tbl_2[ids[:, 2]], tbl_3[ids[:, 3]], tbl_4[ids[:, 4]], tbl_5[ids[:, 5]], tbl_6[ids[:, 6]], tbl_7[ids[:, 7]], tbl_8[ids[:, 8]], tbl_9[ids[:, 9]], tbl_10[ids[:, 10]], tbl_11[ids[:, 11]], tbl_12[ids[:, 12]], tbl_13[ids[:, 13]], tbl_14[ids[:, 14]], tbl_15[ids[:, 15]], tbl_16[ids[:, 16]], tbl_17[ids[:, 17]], tbl_18[ids[:, 18]], tbl_19[ids[:, 19]], tbl_20[ids[:, 20]], tbl_21[ids[:, 21]], tbl_22[ids[:, 22]], tbl_23[ids[:, 23]], tbl_24[ids[:, 24]], tbl_25[ids[:, 25]], tbl_26[ids[:, 26]], tbl_27[ids[:, 27]], tbl_28[ids[:, 28]], tbl_29[ids[:, 29]], tbl_30[ids[:, 30]], tbl_31[ids[:, 31]]], axis=1)
    z = _L0_rec_ref(e, L0_rec_w0, L0_rec_b0, L0_rec_w1, L0_rec_b1)
    z = z.reshape(z.shape[0], -1)
    h = jnp.concatenate([z, dense_ctx], axis=1)
    h = jnp.maximum(h @ W_top1 + b_top1, 0.0)
    h = jnp.maximum(h @ W_top2 + b_top2, 0.0)
    y = h @ W_top3
    return y

_drawn_inputs = setup_inputs


def setup_inputs(seed=0):
    import zlib

    import numpy as np

    out = dict(_drawn_inputs(seed))
    spreads = {'b_top1': (0.0, 0.418), 'b_top2': (0.0, 0.1)}
    factors = {'tbl_0': 8.0,
     'tbl_1': 8.0,
     'tbl_2': 8.0,
     'tbl_3': 8.0,
     'tbl_4': 8.0,
     'tbl_5': 8.0,
     'tbl_6': 8.0,
     'tbl_7': 8.0,
     'tbl_8': 8.0,
     'tbl_9': 8.0,
     'tbl_10': 8.0,
     'tbl_11': 8.0,
     'tbl_12': 8.0,
     'tbl_13': 8.0,
     'tbl_14': 8.0,
     'tbl_15': 8.0,
     'tbl_16': 8.0,
     'tbl_17': 8.0,
     'tbl_18': 8.0,
     'tbl_19': 8.0,
     'tbl_20': 8.0,
     'tbl_21': 8.0,
     'tbl_22': 8.0,
     'tbl_23': 8.0,
     'tbl_24': 8.0,
     'tbl_25': 8.0,
     'tbl_26': 8.0,
     'tbl_27': 8.0,
     'tbl_28': 8.0,
     'tbl_29': 8.0,
     'tbl_30': 8.0,
     'tbl_31': 8.0,
     'L0_rec_w1': 6.603}
    for name, (base, spread) in spreads.items():
        noise = np.random.default_rng([zlib.crc32(name.encode()), seed]).standard_normal(out[name].shape)
        drawn = base * np.exp(spread * noise) if base else spread * noise
        out[name] = jnp.asarray(drawn.astype(out[name].dtype))
    for name, factor in factors.items():
        out[name] = (out[name] * factor).astype(out[name].dtype)
    return out
```

```python
from contextlib import ExitStack

import concourse.bass as bass
from concourse import mybir
import numpy as np

F32 = mybir.dt.float32
F32R = mybir.dt.float32r
I32 = mybir.dt.int32
ALU = mybir.AluOpType
ACT = mybir.ActivationFunctionType
AX_X = mybir.AxisListType.X

P = 128
B, F, D = 512, 32, 64
H = 64
NC = B // P
ND = 4
N = ND * P
G = NC * D // ND
GC = D // ND
T1, T2 = 4, 16
XROWS = 48
BAND = 2 * F + 3
SLOTS = 5
GA = 6
LOADS = 6

P_NAMES = ["P0", "P1"]
Q_NAMES = ["Q%d" % j for j in range(T2 // 2)]
FILLED = Q_NAMES[2:]
LAST = G - 1

MODES = {
    "A": dict(P0="V", P1="F", S="V", Q0="F", Q1="V", Q2="F", Q3="V", Q4="F", Q5="V", Q6="F", Q7="V"),
    "B": dict(P0="V", P1="P", S="V", Q0="P", Q1="V", Q2="P", Q3="P", Q4="V", Q5="P", Q6="F", Q7="P"),
}
V_LAG = 2
LEAD = 3


def mode(g, name):
    return MODES["A" if g < GA else "B"][name]


def pairs(g):
    return (P_NAMES if g < LAST else []) + (Q_NAMES if g >= 0 else [])


def events(kind, g):
    if kind in ("mult", "used"):
        return pairs(g)
    if kind == "hi":
        return [n for n in pairs(g) if mode(g, n) != "F"]
    if kind in ("lo_v", "lo_p"):
        return [n for n in pairs(g) if mode(g, n) == kind[-1].upper()]
    if kind in ("slo_v", "slo_p"):
        return ["S"] if g < LAST and mode(g, "S") == kind[-1].upper() else []
    if kind == "fill":
        return FILLED if g >= 0 else []
    raise ValueError(kind)


def back(g, name, by):
    at, rel = pairs(g).index(name) - by, 0
    while at < 0:
        rel -= 1
        if g + rel < -1:
            return None
        at += len(pairs(g + rel))
    return rel, pairs(g + rel)[at]


def slot(g, name):
    return (sum(len(pairs(i)) for i in range(-1, g)) + pairs(g).index(name)) % SLOTS


class Step:

    def __init__(self, g, reg=None, reg0=0):
        self.g, self.reg, self.reg0 = g, reg, reg0

    def affine(self, value, per):
        return value if self.reg is None else self.reg * (2 * per) + (value - per * self.reg0)

    def count(self, kind, rel=0, name=None):
        g = self.g + rel
        before = sum(len(events(kind, i)) for i in range(-1, g))
        own = events(kind, g)
        value = before + (len(own) if name is None else own.index(name) + 1)
        return self.affine(value, len(events(kind, self.g)))

    def nth(self, rel=0, per=1, off=0):
        return self.affine(per * (self.g + rel + 1) + off, per)


def need(eng, sem, value):
    if not isinstance(value, int) or value > 0:
        eng.wait_ge(sem, value)


def steps(eng, body):
    start, end = GA + 4, LAST - 1
    for g in range(start):
        body(Step(g))
    with eng.Fori(start // 2, end // 2) as turn:
        for u in range(2):
            body(Step(start + u, turn, start))
    for g in range(end, G):
        body(Step(g))


def view(t, offset, dims):
    whole = t[:]
    return bass.AP(tensor=whole.tensor, offset=offset, ap=[list(whole.ap[0])] + [list(d) for d in dims])


def dlrm_tower(nc, dense_ctx, ids, tables, W_top1, b_top1, W_top2, b_top2, W_top3, w0, b0, w1, b1,
               eye, band_const, out):
    with ExitStack() as ctx:
        def sb(name, shape, dt=F32):
            return ctx.enter_context(nc.sbuf_tensor(name, shape, dt))

        def sem(name):
            return ctx.enter_context(nc.semaphore(name))

        emb = sb("emb", [P, F, NC, D])
        idx = sb("idx", [P, NC, F], I32)
        wf = sb("wf", [P, T1 + T2, P])
        wh = sb("wh", [P, T1 + T2, P], F32R)
        wl = sb("wl", [P, T1 + T2, P], F32R)
        wSf = sb("wSf", [P, P])
        wS = sb("wS", [P, P], F32R)
        ident = sb("ident", [P, P])
        bandf = sb("bandf", [P, BAND])
        spread = sb("spread", [P, len(FILLED) * 2, P], F32R)
        bias0 = sb("bias0", [P, 1])
        bias1 = sb("bias1", [P, 1])
        xd = sb("xd", [P, 2, LOADS, N])
        xs = sb("xs", [P, 2, N], F32R)
        xf = sb("xf", [F, N])
        stage = sb("stage", [P, ND, 3, F])
        zf = sb("zf", [P, SLOTS, 2, N])
        zh = sb("zh", [P, SLOTS, 2, N], F32R)
        zl = sb("zl", [P, SLOTS, 2, N], F32R)
        zSf = sb("zSf", [P, N])
        zS = sb("zS", [P, 2, N], F32R)
        hid = sb("hid", [P, 2, N])
        dir1 = sb("dir1", [P, N])
        dir2 = sb("dir2", [P, 2, N])
        acc1 = sb("acc1", [P, NC, N])
        acc2 = sb("acc2", [P, NC, N])
        wt1a = sb("wt1a", [P, B])
        wt1b = sb("wt1b", [P, B])
        wt1c = sb("wt1c", [16, B])
        wt2 = sb("wt2", [P, 4, 256])
        wt3 = sb("wt3", [P, 2])
        bt1 = sb("bt1", [P, 4])
        bt2 = sb("bt2", [P, 2])
        dense = sb("dense", [P, NC, 16])
        denseT = sb("denseT", [16, B])

        xd_flat = xd[:].rearrange("p a t n -> p (a t n)")
        w0_twice = xd_flat[:, 0:2048]
        w0_ext = xd_flat[:, 2048:4096]
        w1_nat = xd_flat[:, 4096:6144]
        zf_flat = zf[:].rearrange("p a t n -> p (a t n)")
        w1_ext = zf_flat[:, 0:4096]
        sym = zf_flat[:, 4096:4096 + 512]
        sym16 = zf_flat[:, 4608:4608 + 128]
        acc2_flat = acc2[:].rearrange("p c n -> p (c n)")
        w1_rot = acc2_flat
        zsum1, zsum2 = zf_flat[:, 0:512], zf_flat[:, 512:1024]
        act1 = zf_flat[:, 1024:3072].rearrange("p (m n) -> p m n", m=4)
        act2 = zf_flat[:, 3072:4096].rearrange("p (m n) -> p m n", m=2)
        yrow = zf_flat[0:1, 4096:4608]

        px = ctx.enter_context(nc.psum_tensor("px", [P, 4, N], F32))
        py1 = ctx.enter_context(nc.psum_tensor("py1", [P, N], F32))
        py2 = ctx.enter_context(nc.psum_tensor("py2", [P, N], F32))
        pt = ctx.enter_context(nc.psum_tensor("pt", [P, ND, P], F32))
        pw = ctx.enter_context(nc.psum_tensor("pw", [P, N], F32))

        x_dram = nc.dram_tensor("x_dram", [2, XROWS, N], F32, kind="Internal").ap()

        ids_in = sem("ids_in")
        consts_in = sem("consts_in")
        cin_in = sem("cin_in")
        top_in = sem("top_in")
        gathered = [sem("gathered%d" % c) for c in range(NC)]
        zeroed = sem("zeroed")
        w_doubled = sem("w_doubled")
        w_turned = sem("w_turned")
        w_high = sem("w_high")
        w_low = sem("w_low")
        s_low = sem("s_low")
        stage_hi = sem("stage_hi")
        stage_lo = sem("stage_lo")
        turned = sem("turned")
        xf_ready = sem("xf_ready")
        xs_ready = sem("xs_ready")
        x_stored = sem("x_stored")
        x_loaded = [sem("x_loaded0"), sem("x_loaded1")]
        mult = sem("mult")
        hi = sem("hi")
        lo_v = sem("lo_v")
        lo_p = sem("lo_p")
        used = sem("used")
        fill = sem("fill")
        s_mult = sem("s_mult")
        s_hi = sem("s_hi")
        slo_v = sem("slo_v")
        slo_p = sem("slo_p")
        y1_ready = sem("y1_ready")
        hid_ready = sem("hid_ready")
        dir1_ready = sem("dir1_ready")
        dir2_ready = sem("dir2_ready")
        acc1_v, acc1_p = sem("acc1_v"), sem("acc1_p")
        acc2_v, acc2_p = sem("acc2_v"), sem("acc2_p")
        zsum_ready = sem("zsum_ready")
        dense_turned, dense_ready = sem("dense_turned"), sem("dense_ready")
        top_mm, top_act = sem("top_mm"), sem("top_act")
        y_ready, y_out = sem("y_ready"), sem("y_out")

        lo_sem = {"V": lo_v, "P": lo_p}
        lo_kind = {"V": "lo_v", "P": "lo_p"}

        def need_low(eng, st, rel, name):
            m = mode(st.g + rel, name)
            need(eng, lo_sem[m], st.count(lo_kind[m], rel, name))

        def need_s_low(eng, st, rel):
            if st.g + rel < -1:
                return
            if mode(st.g + rel, "S") == "V":
                need(eng, slo_v, st.count("slo_v", rel))
            else:
                need(eng, slo_p, st.count("slo_p", rel))

        def pair_tiles(name):
            t = 2 * int(name[1])
            return (t, t) if name[0] == "P" else (T1 + t, t)

        def need_acc1(eng, st, rel):
            if st.g + rel < GA:
                need(eng, acc1_v, st.nth(rel))
            else:
                need(eng, acc1_p, st.nth(rel, off=-GA))

        def need_acc2(eng, st, rel):
            if st.g + rel < GA:
                need(eng, acc2_v, st.nth(rel))
            else:
                need(eng, acc2_p, st.nth(rel, off=-GA))

        def chunk_sum(acc, st, rel):
            if st.reg is None:
                return acc[:, (st.g + rel) // GC, :]
            return acc[:, bass.ds(st.nth(rel - 1) // GC, 1), :].rearrange("p a n -> p (a n)")

        def add_dir2(eng, done, st, rel):
            eng.wait_ge(dir2_ready, st.nth(rel))
            s = chunk_sum(acc2, st, rel)
            if st.g + rel > 0:
                need_acc2(eng, st, rel - 1)
            eng.tensor_tensor(s, s, dir2[:, (st.g + rel) % 2, :], ALU.add).then_inc(done, 1)

        def add_dir1(eng, done, st):
            eng.wait_ge(dir1_ready, st.nth(1))
            s = chunk_sum(acc1, st, 0)
            if st.g > 0:
                need_acc1(eng, st, -1)
            eng.tensor_tensor(s, s, dir1[:], ALU.add).then_inc(done, 2)

        block = ctx.enter_context(nc.Block())

        @block.sync
        def _(sp):
            sp.dma_start(idx[:], ids.rearrange("(c p) f -> p c f", p=P)).then_inc(ids_in, 16)
            sp.dma_start(ident[:], eye).then_inc(consts_in, 16)
            sp.dma_start(bandf[:], band_const).then_inc(consts_in, 16)
            sp.dma_start(w0_twice[:, 0:1024], w0).then_inc(cin_in, 16)
            sp.dma_start(w0_twice[:, 1024:2048], w0).then_inc(cin_in, 16)
            sp.dma_start(w1_nat, w1).then_inc(cin_in, 16)
            sp.dma_start(bias0[:], b0.rearrange("(p a) -> p a", a=1)).then_inc(consts_in, 16)
            sp.dma_start(bias1[:], b1.rearrange("(p a) -> p a", a=1)).then_inc(consts_in, 16)
            for half in range(2):
                sp.dma_start(wt1a[H * half:H * half + H, :], W_top1[0:H, :]).then_inc(top_in, 16)
            sp.dma_start(wt1b[:], W_top1[H:H + P, :]).then_inc(top_in, 16)
            sp.dma_start(wt1c[:], W_top1[H + P:H + P + 16, :]).then_inc(top_in, 16)
            sp.dma_start(wt2[:], W_top2.rearrange("(k p) n -> p k n", p=P)).then_inc(top_in, 16)
            sp.dma_start(wt3[:], W_top3.rearrange("(k p) n -> p (k n)", p=P), allow_slow_non_contiguous=True).then_inc(top_in, 16)
            sp.dma_start(bt1[:], b_top1.rearrange("(k p) -> p k", p=P), allow_slow_non_contiguous=True).then_inc(top_in, 16)
            sp.dma_start(bt2[:], b_top2.rearrange("(k p) -> p k", p=P), allow_slow_non_contiguous=True).then_inc(top_in, 16)
            sp.dma_start(dense[:], dense_ctx.rearrange("(c p) n -> p c n", p=P)).then_inc(top_in, 16)

            def load_x(st, rel):
                s = (st.g + rel) % 2
                sp.wait_ge(xf_ready, st.nth(rel))
                sp.dma_start(x_dram[s, 0:F, :], xf[:]).then_inc(x_stored, 16)
                sp.dma_start(x_dram[s, F:XROWS, :], xf[0:XROWS - F, :]).then_inc(x_stored, 16)
                sp.wait_ge(x_stored, st.nth(rel, 32))
                src = x_dram[s]

                def rows(r, dj):
                    return bass.AP(tensor=src.tensor, offset=src.offset + r * N, ap=[[dj * N, 4], [N, F], [1, N]])

                tiles = [(4, rows(0, 0)), (5, rows(16, 0))] + [(t, rows(4 * t, 1)) for t in range(T1)]
                for t, ap in tiles:
                    sp.dma_start(xd[:, s, t, :], ap).then_inc(x_loaded[s], 16)

            sp.wait_ge(w_turned, 6)
            load_x(Step(0), 0)
            load_x(Step(1), 0)

            def step(st):
                if st.g + 2 < G:
                    load_x(st, 2)

            steps(sp, step)
            sp.wait_ge(y_ready, 1)
            sp.dma_start(out.rearrange("b a -> a b"), yrow).then_inc(y_out, 16)
            sp.wait_ge(y_out, 16)

        @block.gpsimd
        def _(pool):
            pool.wait_ge(ids_in, 16)
            for c in range(NC):
                for f in range(F):
                    pool.indirect_dma_start(
                        out=emb[:, f, c, :], out_offset=None, in_=tables[f],
                        in_offset=bass.IndirectOffsetOnAxis(ap=idx[:, c, f:f + 1], axis=0),
                    ).then_inc(gathered[c], 16)

            def low(st, rel, name):
                if mode(st.g + rel, name) != "P":
                    return
                s = slot(st.g + rel, name)
                pool.wait_ge(hi, st.count("hi", rel, name))
                pool.tensor_tensor(zl[:, s], zf[:, s], zh[:, s].bitcast(F32), ALU.subtract).then_inc(lo_p, 1)

            def step(st):
                if st.g < GA:
                    return
                for name in pairs(st.g):
                    low(st, 0, name)
                    if name == "P1" and mode(st.g, "S") == "P":
                        pool.wait_ge(s_hi, st.nth(1))
                        s = (st.g + 1) % 2
                        pool.tensor_tensor(zS[H:P, s], zSf[H:P], zS[H:P, s].bitcast(F32),
                                           ALU.subtract).then_inc(slo_p, 1)
                    if name == "Q2" and st.g > GA:
                        add_dir2(pool, acc2_p, st, -1)
                    if name == "Q6" and st.g % 2 == 0 and st.g < LAST:
                        add_dir1(pool, acc1_p, st)

            pool.wait_ge(acc1_v, GA)
            pool.wait_ge(acc2_v, GA)
            steps(pool, step)
            add_dir2(pool, acc2_p, Step(LAST), 0)

        @block.scalar
        def _(act):
            banks = [px[:, 0], px[:, 1], px[:, 2], px[:, 3], pw[:]]
            for b in range(5):
                act.wait_ge(w_turned, b + 1)
                dst = slice(4 * b, 4 * b + 4)
                act.activation(wh[:, dst].rearrange("p t n -> p (t n)"), banks[b], ACT.Copy).then_inc(w_high, 1)
                act.activation(wf[:, dst].rearrange("p t n -> p (t n)"), banks[b], ACT.Copy).then_inc(w_high, 1)
            act.wait_ge(w_turned, 6)
            act.activation(wS[:], pt[:, 0, :], ACT.Copy).then_inc(w_high, 1)
            act.activation(wSf[:], pt[:, 0, :], ACT.Copy).then_inc(w_high, 1)
            act.wait_ge(consts_in, 64)
            act.wait_ge(zeroed, 1)

            def stage_x(st, rel):
                if st.g + rel >= 1:
                    act.wait_ge(turned, st.nth(rel - 1))
                cols = emb[:].rearrange("p f c d -> p f (c d)")[:, :, bass.ds(st.nth(rel - 1, ND), ND)].rearrange("p f d -> p d f")
                act.activation(stage[:, :, 2, :], cols, ACT.Copy).then_inc(stage_hi, 1)
                act.activation(stage[:, :, 0, :].bitcast(F32R), cols, ACT.Copy).then_inc(stage_hi, 1)

            def copy_xf(st, rel):
                act.wait_ge(turned, st.nth(rel))
                if st.g + rel >= 1:
                    act.wait_ge(x_stored, st.nth(rel - 1, 32))
                act.activation(xf[:], pt[2 * F:3 * F].rearrange("p a n -> p (a n)"), ACT.Copy).then_inc(xf_ready, 1)

            def copy_xs(st, rel):
                if st.g + rel >= 2:
                    act.wait_ge(fill, st.count("fill", rel - 2))
                act.activation(xs[0:2 * F, (st.g + rel) % 2], pt[0:2 * F].rearrange("p a n -> p (a n)"),
                               ACT.Copy).then_inc(xs_ready, 1)

            def high(st, name):
                if mode(st.g, name) == "F":
                    return
                s = slot(st.g, name)
                act.wait_ge(mult, st.count("mult", 0, name))
                prev = back(st.g, name, SLOTS)
                if prev is not None:
                    act.wait_ge(used, st.count("used", *prev))
                act.activation(zh[:, s], zf[:, s], ACT.Copy).then_inc(hi, 1)

            def high_s(st):
                act.wait_ge(s_mult, st.nth(1))
                if st.g >= 1:
                    act.wait_ge(y1_ready, st.nth(-1))
                act.activation(zS[:, (st.g + 1) % 2], zSf[:], ACT.Copy).then_inc(s_hi, 1)

            def finish_1(st):
                s = (st.g + 1) % 2
                act.wait_ge(y1_ready, st.nth(1))
                if st.g >= 1:
                    act.wait_ge(mult, st.count("mult", -1, "Q7"))
                act.activation(hid[0:H, s], py1[0:H], ACT.Relu, bias=bias0[0:H]).then_inc(hid_ready, 1)
                act.activation(hid[H:P, s], py1[0:H], ACT.Relu, bias=bias0[0:H]).then_inc(hid_ready, 1)
                if s == 0 and st.g >= 1:
                    need_acc1(act, st, 0)
                act.activation(dir1[H * s:H * s + H], py1[H:P], ACT.Relu, bias=bias0[H:P]).then_inc(dir1_ready, 1)

            def finish_2(st, rel):
                act.wait_ge(used, st.count("used", rel, "Q7"))
                if st.g + rel >= 2:
                    need_acc2(act, st, rel - 2)
                act.activation(dir2[:, (st.g + rel) % 2], py2[:], ACT.Relu, bias=bias1[:]).then_inc(dir2_ready, 1)

            act.wait_ge(gathered[0], 16 * F)
            act.wait_ge(s_low, 3)
            for k in range(2):
                stage_x(Step(k), 0)
                copy_xf(Step(k), 0)
                copy_xs(Step(k), 0)
            start = Step(-1)
            for name in P_NAMES:
                high(start, name)
            high_s(start)
            finish_1(start)

            def step(st):
                if st.g == GA:
                    for c in range(1, NC):
                        act.wait_ge(gathered[c], 16 * F)
                for name in pairs(st.g):
                    high(st, name)
                    if name == "P1":
                        high_s(st)
                        if st.g + 2 < G:
                            stage_x(st, 2)
                    if name == "Q1" and st.g >= 1:
                        finish_2(st, -1)
                    if name == "Q4" and st.g < LAST:
                        finish_1(st)
                    if name == "Q6" and st.g + 2 < G:
                        copy_xf(st, 2)
                    if name == "Q7" and st.g + 2 < G:
                        copy_xs(st, 2)

            steps(act, step)
            finish_2(Step(LAST), 0)

            for m in range(4):
                act.wait_ge(top_mm, m + 1)
                act.activation(act1[:, m], px[:, m], ACT.Relu, bias=bt1[:, m:m + 1]).then_inc(top_act, 1)
            for m in range(2):
                act.wait_ge(top_mm, 4 + m + 1)
                act.activation(act2[:, m], (py1, py2)[m][:], ACT.Relu, bias=bt2[:, m:m + 1]).then_inc(top_act, 1)
            act.wait_ge(top_mm, 7)
            act.activation(yrow, pw[0:1, :], ACT.Copy).then_inc(y_ready, 1)

        @block.vector
        def _(dve):
            dve.memset(xs[2 * F:P].bitcast(F32), 0.0).then_inc(zeroed, 1)
            dve.memset(acc1[:], 0.0).then_inc(zeroed, 1)
            dve.wait_ge(cin_in, 48)
            dve.tensor_copy(w0_ext.rearrange("p (h a f) -> p h a f", a=2, f=F),
                            w0_twice[:, 0:1024].rearrange("p (h a f) -> p h a f", a=1, f=F)
                            .to_broadcast([P, F, 2, F])).then_inc(w_doubled, 1)
            dve.tensor_copy(w1_ext.rearrange("p (h a f) -> p h a f", a=2, f=F),
                            w1_nat.rearrange("p (h a f) -> p h a f", a=1, f=F)
                            .to_broadcast([P, H, 2, F])).then_inc(w_doubled, 1)
            dve.wait_ge(w_doubled, 2)
            straight = view(xd, 2048, [[1, 16], [2 * F + 1, F]])
            crossed = view(xd, 0, [[F, 16], [F + 1, F]])
            dve.tensor_tensor(sym.rearrange("p (r i) -> p r i", i=F), straight, crossed, ALU.add).then_inc(w_doubled, 1)
            dve.wait_ge(w_doubled, 3)
            dve.tensor_copy(sym[:, 0:F], view(xd, 2048, [[2 * F + 1, F]])).then_inc(w_doubled, 1)
            dve.tensor_copy(sym16.rearrange("p (j i) -> p j i", i=F),
                            view(xd, 2048 + 16, [[0, 4], [2 * F + 1, F]])).then_inc(w_doubled, 1)
            for odd in range(2):
                dve.tensor_copy(w1_rot[:, 1024 * odd:1024 * odd + 1024].rearrange("p (s u i) -> p s u i", u=2, i=F),
                                view(zf, odd, [[2, 16], [2 * F * F + 1, 2], [2 * F + 1, F]])).then_inc(w_doubled, 1)
            dve.wait_ge(consts_in, 64)
            t = 2 * int(FILLED[0][1])
            for dst, n, rot in ((0, 8 - t, 4 * t), (8 - t, 8, 1)):
                dve.tensor_copy(spread[:, dst:dst + n].rearrange("p t (j i) -> p t j i", i=F),
                                view(bandf, rot, [[4, n], [1, 4], [1, F]])).then_inc(w_doubled, 1)
            for b in range(5):
                dst = slice(4 * b, 4 * b + 4)
                dve.wait_ge(w_high, 2 * b + 2)
                dve.tensor_tensor(wl[:, dst], wf[:, dst], wh[:, dst].bitcast(F32), ALU.subtract).then_inc(w_low, 1)
            dve.wait_ge(w_high, 12)
            dve.tensor_tensor(wS[32:64], wSf[32:64], wS[32:64].bitcast(F32), ALU.subtract).then_inc(s_low, 1)
            dve.tensor_tensor(wS[96:128], wSf[96:128], wS[96:128].bitcast(F32), ALU.subtract).then_inc(s_low, 1)
            dve.wait_ge(top_in, 16 * 9)
            dve.wait_ge(s_low, 2)
            dve.wait_ge(dense_turned, 1)
            dve.tensor_copy(denseT[:], pt[0:16].rearrange("p a n -> p (a n)")).then_inc(s_low, 1)

            def stage_low(st, rel):
                dve.wait_ge(stage_hi, st.nth(rel, 2))
                dve.tensor_tensor(stage[:, :, 1, :], stage[:, :, 2, :], stage[:, :, 0, :],
                                  ALU.subtract).then_inc(stage_lo, 1)

            def slot_free(st, name):
                prev = back(st.g, name, SLOTS)
                if prev is None:
                    return
                if mode(st.g + prev[0], prev[1]) == "F":
                    dve.wait_ge(used, st.count("used", *prev))
                else:
                    need_low(dve, st, *prev)

            def products(st, name):
                s = slot(st.g, name)
                _, t = pair_tiles(name)
                slot_free(st, name)
                if name[0] == "P":
                    x = (st.g + 1) % 2
                    if name == "P0":
                        dve.wait_ge(x_loaded[x], st.nth(1, 8 * LOADS, 8 * LOADS * (1 - x)))
                    left, right = xd[:, x, t:t + 2, :], xd[:, x, 4:5, :]
                else:
                    if name == "Q0":
                        dve.wait_ge(hid_ready, st.nth(0, 2))
                    if name in FILLED:
                        dve.wait_ge(fill, st.count("fill", 0, name))
                        left = px[:, t % 4:t % 4 + 2, :]
                    else:
                        left = xd[:, st.g % 2, t:t + 2, :]
                    right = hid[:, st.g % 2:st.g % 2 + 1, :]
                dve.tensor_tensor(zf[:, s], left, right.to_broadcast([P, 2, N]), ALU.mult).then_inc(mult, 1)

            def products_s(st):
                x = (st.g + 1) % 2
                need_s_low(dve, st, -1)
                dve.tensor_tensor(zSf[:], xd[:, x, 5, :], xd[:, x, 4, :], ALU.mult).then_inc(s_mult, 1)

            def low(st, rel, name):
                if mode(st.g + rel, name) != "V":
                    return
                s = slot(st.g + rel, name)
                dve.wait_ge(hi, st.count("hi", rel, name))
                dve.tensor_tensor(zl[:, s], zf[:, s], zh[:, s].bitcast(F32), ALU.subtract).then_inc(lo_v, 1)

            def low_s(st):
                if mode(st.g, "S") == "V":
                    s = (st.g + 1) % 2
                    dve.wait_ge(s_hi, st.nth(1))
                    dve.tensor_tensor(zS[H:P, s], zSf[H:P], zS[H:P, s].bitcast(F32), ALU.subtract).then_inc(slo_v, 1)

            stage_low(Step(0), 0)
            stage_low(Step(1), 0)
            dve.wait_ge(w_turned, 6)
            dve.memset(acc2[:], 0.0).then_inc(zeroed, 1)
            dve.wait_ge(zeroed, 3)
            start = Step(-1)
            products(start, "P0")
            products(start, "P1")
            products_s(start)
            low_s(start)

            def step(st):
                for name in pairs(st.g):
                    products(st, name)
                    if name == "P1":
                        products_s(st)
                    behind = back(st.g, name, V_LAG)
                    if behind is not None:
                        low(st, *behind)
                    if name == "Q0" and st.g < LAST:
                        low_s(st)
                    if name == "Q1" and st.g + 2 < G:
                        stage_low(st, 2)
                    if name == "Q2" and 1 <= st.g <= GA:
                        add_dir2(dve, acc2_v, st, -1)
                    if name == "Q6" and st.g % 2 == 0 and st.g < GA:
                        add_dir1(dve, acc1_v, st)

            steps(dve, step)
            for name in pairs(LAST)[-V_LAG:]:
                low(Step(LAST), 0, name)

            dve.wait_ge(used, Step(LAST).count("used"))
            dve.wait_ge(acc1_p, G - GA)
            dve.tensor_reduce(zsum1.rearrange("p (c b) -> p c b", b=P),
                              acc1[:].rearrange("p c (d b) -> p c b d", d=ND), AX_X, ALU.add).then_inc(zsum_ready, 1)
            dve.wait_ge(acc2_p, G - GA)
            dve.tensor_reduce(zsum2.rearrange("p (c b) -> p c b", b=P),
                              acc2[:].rearrange("p c (d b) -> p c b d", d=ND), AX_X, ALU.add).then_inc(zsum_ready, 1)

        @block.tensor
        def _(pe):
            pe.wait_ge(consts_in, 64)
            pe.wait_ge(w_doubled, 9)
            banks = [px[:, 0], px[:, 1], px[:, 2], px[:, 3], pw[:]]
            for t in range(T1 + T2):
                src = sym[:, P * t:P * t + P] if t < T1 else w1_rot[:, P * (t - T1):P * (t - T1) + P]
                tr = pe.transpose(banks[t // 4][:, P * (t % 4):P * (t % 4) + P], src, ident[:])
                if t % 4 == 3:
                    tr.then_inc(w_turned, 1)
            pe.transpose(pt[:, 0, :], sym16, ident[:]).then_inc(w_turned, 1)
            pe.wait_ge(top_in, 16 * 9)
            pe.wait_ge(s_low, 2)
            for c in range(NC):
                tr = pe.transpose(pt[0:16, c, :], dense[:, c, :], ident[:])
            tr.then_inc(dense_turned, 1)

            def turn_x(st, rel):
                pe.wait_ge(stage_lo, st.nth(rel))
                if st.g + rel >= 1:
                    pe.wait_ge(xs_ready, st.nth(rel - 1))
                for d in range(ND):
                    tr = pe.transpose(pt[0:3 * F, d, :], stage[:, d].rearrange("p a f -> p (a f)"), ident[:])
                tr.then_inc(turned, 1)

            def fill_x(st, name):
                _, t = pair_tiles(name)
                if name == FILLED[0]:
                    pe.wait_ge(xs_ready, st.nth(0))
                if name in FILLED[:2]:
                    if st.g >= 1:
                        pe.wait_ge(mult, st.count("mult", -1, FILLED[FILLED.index(name) - 2]))
                else:
                    pe.wait_ge(mult, st.count("mult", 0, FILLED[FILLED.index(name) - 2]))
                for h in range(2):
                    mm = pe.matmul(px[:, (t + h) % 4, :], spread[:, t + h - 2 * int(FILLED[0][1])], xs[:, st.g % 2],
                                   start=True, stop=True)
                mm.then_inc(fill, 1)

            def layer(st, name):
                s = slot(st.g, name)
                w, _ = pair_tiles(name)
                bank = py1 if name[0] == "P" else py2
                first, last = name in ("P0", "Q0"), name == "Q7"
                if name == "P0" and st.g >= 0:
                    pe.wait_ge(dir1_ready, st.nth(0))
                if name == "Q0" and st.g >= 1:
                    pe.wait_ge(dir2_ready, st.nth(-1))
                if mode(st.g, name) == "F":
                    pe.wait_ge(mult, st.count("mult", 0, name))
                    for h in range(2):
                        mm = pe.matmul(bank[:], wf[:, w + h], zf[:, s, h], start=first and h == 0, stop=last and h == 1)
                else:
                    pe.wait_ge(hi, st.count("hi", 0, name))
                    for h in range(2):
                        pe.matmul(bank[:], wh[:, w + h], zh[:, s, h], start=first and h == 0, stop=False)
                        pe.matmul(bank[:], wl[:, w + h], zh[:, s, h], start=False, stop=False)
                    need_low(pe, st, 0, name)
                    for h in range(2):
                        mm = pe.matmul(bank[:], wh[:, w + h], zl[:, s, h], start=False, stop=last and h == 1)
                mm.then_inc(used, 1)

            def layer_s(st):
                need_s_low(pe, st, 0)
                pe.matmul(py1[:], wS[:], zS[:, (st.g + 1) % 2], start=False, stop=True).then_inc(y1_ready, 1)

            pe.wait_ge(zeroed, 2)
            pe.wait_ge(s_low, 3)
            turn_x(Step(0), 0)
            pe.wait_ge(xf_ready, 1)
            turn_x(Step(1), 0)
            pe.wait_ge(w_low, 5)
            start = Step(-1)
            layer(start, "P0")
            layer(start, "P1")
            layer_s(start)

            def step(st):
                names = pairs(st.g)
                order = (P_NAMES + Q_NAMES)
                for name in order:
                    at = order.index(name) + LEAD
                    if name == "P0":
                        for early in order[:at + 1]:
                            if early in FILLED:
                                fill_x(st, early)
                    elif at < len(order) and order[at] in FILLED:
                        fill_x(st, order[at])
                    if name in names:
                        layer(st, name)
                    if name == "P1" and st.g < LAST:
                        layer_s(st)
                    if name == "Q1" and st.g + 2 < G:
                        turn_x(st, 2)

            steps(pe, step)

            pe.wait_ge(zsum_ready, 2)
            for m in range(4):
                cols = slice(P * m, P * m + P)
                pe.matmul(px[:, m], wt1a[:, cols], zsum1, start=True, stop=False)
                pe.matmul(px[:, m], wt1b[:, cols], zsum2, start=False, stop=False)
                pe.matmul(px[:, m], wt1c[:, cols], denseT[:], start=False, stop=True).then_inc(top_mm, 1)
            for m in range(2):
                for k in range(4):
                    if m == 0:
                        pe.wait_ge(top_act, k + 1)
                    mm = pe.matmul((py1, py2)[m][:], wt2[:, k, P * m:P * m + P], act1[:, k], start=k == 0, stop=k == 3)
                mm.then_inc(top_mm, 1)
            for k in range(2):
                pe.wait_ge(top_act, 4 + k + 1)
                mm = pe.matmul(pw[0:1, :], wt3[:, k:k + 1], act2[:, k], start=k == 0, stop=k == 1)
            mm.then_inc(top_mm, 1)


_SMALL = ["W_top1", "b_top1", "W_top2", "b_top2", "W_top3", "L0_rec_w0", "L0_rec_b0", "L0_rec_w1", "L0_rec_b1"]
_INS = ["dense_ctx", "ids"] + ["tbl_%d" % f for f in range(F)] + _SMALL


def kernel(**inputs):
    import concourse.bacc as _bacc
    from concourse.bass_utils import run_bass_kernel_spmd as _run

    nc = _bacc.Bacc("TRN2", target_bir_lowering=False, num_devices=1)
    arrays, args = {}, {}
    given = {name: np.ascontiguousarray(inputs[name]) for name in _INS}
    given["eye"] = np.eye(P, dtype=np.float32)
    row, col = np.arange(P)[:, None], np.arange(BAND)[None, :]
    given["band"] = ((row < 2 * F) & (row % F == col % F)).astype(np.float32)
    for name, a in given.items():
        arrays["in_" + name] = a
        args[name] = nc.dram_tensor("in_" + name, a.shape, mybir.dt.from_np(a.dtype), kind="ExternalInput").ap()
    out = nc.dram_tensor("out_0", (B, 1), F32, kind="ExternalOutput").ap()
    dlrm_tower(nc, args["dense_ctx"], args["ids"], [args["tbl_%d" % f] for f in range(F)],
               *[args[name] for name in _SMALL], args["eye"], args["band"], out)
    r = _run(nc, [arrays], core_ids=[0])
    return r.results[0]["out_0"]
```

```python
from contextlib import ExitStack

import concourse.bass as bass
from concourse import mybir
import numpy as np

F32 = mybir.dt.float32
F32R = mybir.dt.float32r
I32 = mybir.dt.int32
ALU = mybir.AluOpType
ACT = mybir.ActivationFunctionType
AX_X = mybir.AxisListType.X

P = 128
B, F, D = 512, 32, 64
H = 64
NC = B // P
ND = 4
N = ND * P
G = NC * D // ND
GC = D // ND
T1, T2 = 4, 16
TL = 8
BAND = 2 * F + 3
SLOTS = 5
GA = 4

P_NAMES = ["P0", "P1"]
Q_NAMES = ["Q%d" % j for j in range(T2 // 2)]
FILLED = Q_NAMES[TL // 2:]
LAST = G - 1

MODES = {
    "A": dict(P0="F", P1="F", S="V", Q0="F", Q1="V", Q2="F", Q3="V", Q4="F", Q5="V", Q6="F", Q7="F"),
    0: dict(P0="P", P1="V", S="V", Q0="P", Q1="P", Q2="V", Q3="P", Q4="P", Q5="V", Q6="F", Q7="P"),
    1: dict(P0="F", P1="P", S="V", Q0="P", Q1="P", Q2="V", Q3="P", Q4="V", Q5="P", Q6="P", Q7="F"),
    "Z": dict(Q0="P", Q1="P", Q2="V", Q3="P", Q4="V", Q5="P", Q6="V", Q7="V"),
}
WHOLE = [n for n in P_NAMES + Q_NAMES if any(m.get(n) == "F" for m in MODES.values())]
V_LAG = 2
AFTER = dict(turn_x="P0", copy_xf="Q2", copy_xs="Q7", stage_low="P1", finish_1="Q4", finish_2="Q1",
             add_dir1="Q6", add_dir2="Q2")
TOP_AFTER = ["Q2", "Q5", "Q7"]
LEAD = 5


def mode(g, name):
    return "V" if g < 0 else MODES["A" if g < GA else "Z" if g == LAST else g % 2][name]


def pairs(g):
    return (P_NAMES if g < LAST else []) + (Q_NAMES if g >= 0 else [])


def events(kind, g):
    if kind in ("mult", "used"):
        return pairs(g)
    if kind == "hi":
        return [n for n in pairs(g) if mode(g, n) != "F"]
    if kind in ("lo_v", "lo_p"):
        return [n for n in pairs(g) if mode(g, n) == kind[-1].upper()]
    if kind in ("slo_v", "slo_p"):
        return ["S"] if g < LAST and mode(g, "S") == kind[-1].upper() else []
    if kind == "fill":
        return FILLED if g >= 0 else []
    raise ValueError(kind)


def back(g, name, by):
    at, rel = pairs(g).index(name) - by, 0
    while at < 0:
        rel -= 1
        if g + rel < -1:
            return None
        at += len(pairs(g + rel))
    return rel, pairs(g + rel)[at]


def slot(g, name):
    return (sum(len(pairs(i)) for i in range(-1, g)) + pairs(g).index(name)) % SLOTS


class Step:

    def __init__(self, g, reg=None, reg0=0):
        self.g, self.reg, self.reg0 = g, reg, reg0

    def affine(self, value, per_turn):
        return value if self.reg is None else self.reg * per_turn + (value - per_turn * (self.reg0 // 2))

    def count(self, kind, rel=0, name=None):
        g = self.g + rel
        before = sum(len(events(kind, i)) for i in range(-1, g))
        own = events(kind, g)
        value = before + (len(own) if name is None else own.index(name) + 1)
        return self.affine(value, len(events(kind, self.g)) + len(events(kind, self.g + 1)))

    def nth(self, rel=0, per=1, off=0):
        return self.affine(per * (self.g + rel + 1) + off, 2 * per)


def need(eng, sem, value):
    if not isinstance(value, int) or value > 0:
        eng.wait_ge(sem, value)


def steps(eng, body):
    start, end = GA + 4, LAST - 3
    for g in range(start):
        body(Step(g))
    with eng.Fori(start // 2, end // 2) as turn:
        for u in range(2):
            body(Step(start + u, turn, start))
    for g in range(end, G):
        body(Step(g))


def view(t, offset, dims):
    whole = t[:]
    return bass.AP(tensor=whole.tensor, offset=offset, ap=[list(whole.ap[0])] + [list(d) for d in dims])


def dlrm_tower(nc, dense_ctx, ids, tables, W_top1, b_top1, W_top2, b_top2, W_top3, w0, b0, w1, b1,
               eye, band_const, out):
    with ExitStack() as ctx:
        def sb(name, shape, dt=F32):
            return ctx.enter_context(nc.sbuf_tensor(name, shape, dt))

        def sem(name):
            return ctx.enter_context(nc.semaphore(name))

        emb = sb("emb", [P, F, NC, D])
        idx = sb("idx", [P, NC, F], I32)
        wh = sb("wh", [P, T1 + T2, P], F32R)
        wl = sb("wl", [P, T1 + T2, P], F32R)
        wf = sb("wf", [P, 2 * len(WHOLE), P])
        wSf = sb("wSf", [P, P])
        wS = sb("wS", [P, P], F32R)
        ident = sb("ident", [P, P])
        bandf = sb("bandf", [P, BAND])
        spread = sb("spread", [P, T2 - TL, P], F32R)
        bias0 = sb("bias0", [P, 1])
        bias1 = sb("bias1", [P, 1])
        xd = sb("xd", [P, 2, T1 + 2, N])
        xe = sb("xe", [P, TL - T1, N])
        xs = sb("xs", [P, 2, N], F32R)
        xf = sb("xf", [F, N])
        stage = sb("stage", [P, ND, 3, F])
        zf = sb("zf", [P, SLOTS, 2, N])
        zh = sb("zh", [P, SLOTS, 2, N], F32R)
        zl = sb("zl", [P, SLOTS, 2, N], F32R)
        zSf = sb("zSf", [P, N])
        zS = sb("zS", [P, N], F32R)
        hid = sb("hid", [P, 2, N])
        dir1 = sb("dir1", [P, N])
        dir2 = sb("dir2", [P, 2, N])
        acc1 = sb("acc1", [P, NC, N])
        acc2 = sb("acc2", [P, NC, N])
        wt1a = sb("wt1a", [P, B])
        wt1b = sb("wt1b", [P, B])
        wt1c = sb("wt1c", [16, B])
        wt2 = sb("wt2", [P, 4, 256])
        wt3 = sb("wt3", [P, 2])
        bt1 = sb("bt1", [P, 4])
        bt2 = sb("bt2", [P, 2])
        dense = sb("dense", [P, NC, 16])
        denseT = sb("denseT", [16, B])

        xd_flat = xd[:].rearrange("p a t n -> p (a t n)")
        w0_twice = xd_flat[:, 0:2048]
        w0_ext = xd_flat[:, 2048:4096]
        w1_nat = xd_flat[:, 4096:6144]
        zf_flat = zf[:].rearrange("p a t n -> p (a t n)")
        w1_ext = zf_flat[:, 0:4096]
        sym = zf_flat[:, 4096:4096 + 512]
        sym16 = zf_flat[:, 4608:4608 + 128]
        acc2_flat = acc2[:].rearrange("p c n -> p (c n)")
        w1_rot = acc2_flat
        emb_flat = emb[:].rearrange("p f c d -> p (f c d)")
        zsum = emb_flat[:, 0:1024].rearrange("p (a n) -> p a n", a=2)
        act1 = emb_flat[:, 1024:3072].rearrange("p (m n) -> p m n", m=4)
        act2 = emb_flat[:, 3072:4096].rearrange("p (m n) -> p m n", m=2)
        yrow = emb_flat[0:1, 4096:4608]

        px = ctx.enter_context(nc.psum_tensor("px", [P, 4, N], F32))
        py1 = ctx.enter_context(nc.psum_tensor("py1", [P, N], F32))
        py2 = ctx.enter_context(nc.psum_tensor("py2", [P, N], F32))
        pt = ctx.enter_context(nc.psum_tensor("pt", [P, 2, ND, P], F32))
        pw = pt[:, 1].rearrange("p a n -> p (a n)")
        banks = [px[:, 0], px[:, 1], px[:, 2], px[:, 3], pw]
        top1 = [py1[:], pt[:, 0].rearrange("p a n -> p (a n)"), pw, px[:, 3]]
        top2 = [px[:, 0], px[:, 1]]

        x_dram = nc.dram_tensor("x_dram", [G, 2 * F, N], F32, kind="Internal")

        ids_in = sem("ids_in")
        consts_in = sem("consts_in")
        cin_in = sem("cin_in")
        top_in = sem("top_in")
        gathered = [sem("gathered%d" % c) for c in range(NC)]
        zeroed = sem("zeroed")
        w_doubled = sem("w_doubled")
        w_turned = sem("w_turned")
        w_high = sem("w_high")
        w_low = sem("w_low")
        s_low = sem("s_low")
        stage_hi = sem("stage_hi")
        stage_lo = sem("stage_lo")
        turned = sem("turned")
        xf_ready = sem("xf_ready")
        xs_ready = sem("xs_ready")
        x_stored = sem("x_stored")
        x_loaded = [sem("x_loaded0"), sem("x_loaded1")]
        xe_loaded = sem("xe_loaded")
        mult = sem("mult")
        hi = sem("hi")
        lo_v = sem("lo_v")
        lo_p = sem("lo_p")
        used = sem("used")
        fill = sem("fill")
        s_mult = sem("s_mult")
        s_hi = sem("s_hi")
        slo_v = sem("slo_v")
        slo_p = sem("slo_p")
        y1_ready = sem("y1_ready")
        hid_ready = sem("hid_ready")
        dir1_ready = sem("dir1_ready")
        dir2_ready = sem("dir2_ready")
        acc1_v, acc1_p = sem("acc1_v"), sem("acc1_p")
        acc2_v, acc2_p = sem("acc2_v"), sem("acc2_p")
        zsum_ready = sem("zsum_ready")
        dense_turned, dense_ready = sem("dense_turned"), sem("dense_ready")
        top_mm, top_act = sem("top_mm"), sem("top_act")
        y_ready, y_out = sem("y_ready"), sem("y_out")

        lo_sem = {"V": lo_v, "P": lo_p}
        lo_kind = {"V": "lo_v", "P": "lo_p"}

        def need_low(eng, st, rel, name):
            m = mode(st.g + rel, name)
            need(eng, lo_sem[m], st.count(lo_kind[m], rel, name))

        def need_s_low(eng, st, rel):
            if st.g + rel < -1:
                return
            if mode(st.g + rel, "S") == "V":
                need(eng, slo_v, st.count("slo_v", rel))
            else:
                need(eng, slo_p, st.count("slo_p", rel))

        def pair_tiles(name):
            t = 2 * int(name[1])
            return (t, t) if name[0] == "P" else (T1 + t, t)

        def need_acc1(eng, st, rel):
            if st.g + rel < GA:
                need(eng, acc1_v, st.nth(rel))
            else:
                need(eng, acc1_p, st.nth(rel, off=-GA))

        def need_acc2(eng, st, rel):
            if st.g + rel < GA:
                need(eng, acc2_v, st.nth(rel))
            else:
                need(eng, acc2_p, st.nth(rel, off=-GA))

        def chunk_sum(acc, st, rel):
            if st.reg is None:
                return acc[:, (st.g + rel) // GC, :]
            return acc[:, bass.ds(st.nth(rel - 1) // GC, 1), :].rearrange("p a n -> p (a n)")

        def add_dir2(eng, done, st, rel):
            eng.wait_ge(dir2_ready, st.nth(rel))
            s = chunk_sum(acc2, st, rel)
            if st.g + rel > 0:
                need_acc2(eng, st, rel - 1)
            eng.tensor_tensor(s, s, dir2[:, (st.g + rel) % 2, :], ALU.add).then_inc(done, 1)

        def add_dir1(eng, done, st):
            eng.wait_ge(dir1_ready, st.nth(1))
            s = chunk_sum(acc1, st, 0)
            if st.g > 0:
                need_acc1(eng, st, -1)
            eng.tensor_tensor(s, s, dir1[:], ALU.add).then_inc(done, 2)

        block = ctx.enter_context(nc.Block())

        @block.sync
        def _(sp):
            sp.dma_start(idx[:], ids.rearrange("(c p) f -> p c f", p=P)).then_inc(ids_in, 16)
            sp.dma_start(ident[:], eye).then_inc(consts_in, 16)
            sp.dma_start(bandf[:], band_const).then_inc(consts_in, 16)
            sp.dma_start(w0_twice[:, 0:1024], w0).then_inc(cin_in, 16)
            sp.dma_start(w0_twice[:, 1024:2048], w0).then_inc(cin_in, 16)
            sp.dma_start(w1_nat, w1).then_inc(cin_in, 16)
            sp.dma_start(bias0[:], b0.rearrange("(p a) -> p a", a=1)).then_inc(consts_in, 16)
            sp.dma_start(bias1[:], b1.rearrange("(p a) -> p a", a=1)).then_inc(consts_in, 16)
            for half in range(2):
                sp.dma_start(wt1a[H * half:H * half + H, :], W_top1[0:H, :]).then_inc(top_in, 16)
            sp.dma_start(wt1b[:], W_top1[H:H + P, :]).then_inc(top_in, 16)
            sp.dma_start(wt1c[:], W_top1[H + P:H + P + 16, :]).then_inc(top_in, 16)
            sp.dma_start(wt2[:], W_top2.rearrange("(k p) n -> p k n", p=P)).then_inc(top_in, 16)
            sp.dma_start(wt3[:], W_top3.rearrange("(k p) n -> p (k n)", p=P), allow_slow_non_contiguous=True).then_inc(top_in, 16)
            sp.dma_start(bt1[:], b_top1.rearrange("(k p) -> p k", p=P), allow_slow_non_contiguous=True).then_inc(top_in, 16)
            sp.dma_start(bt2[:], b_top2.rearrange("(k p) -> p k", p=P), allow_slow_non_contiguous=True).then_inc(top_in, 16)
            sp.dma_start(dense[:], dense_ctx.rearrange("(c p) n -> p c n", p=P)).then_inc(top_in, 16)

            def store_x(st, rel):
                sp.wait_ge(xf_ready, st.nth(rel))
                for half in range(2):
                    dst = x_dram[bass.ds(st.nth(rel - 1), 1), F * half:F * half + F, :].rearrange("a f n -> (a f) n")
                    sp.dma_start(dst, xf[:]).then_inc(x_stored, 16)

            def rows(k, r, dj):
                src = x_dram[bass.ds(k, 1), r:r + 1, :]
                return bass.AP(tensor=src.tensor, offset=src.offset, ap=[[dj * N, 4], [N, F], [1, N]])

            def load_x(st, rel):
                s, k = (st.g + rel) % 2, st.nth(rel - 1)
                if st.g + rel == 2:
                    sp.wait_ge(s_mult, 1)
                sp.wait_ge(x_stored, st.nth(rel, 32))
                sp.dma_start(xd[:, s, T1, :], rows(k, 0, 0)).then_inc(x_loaded[s], 16)
                sp.dma_start(xd[:, s, T1 + 1, :], rows(k, 16, 0)).then_inc(x_loaded[s], 16)
                if st.g + rel >= 2:
                    sp.wait_ge(mult, st.count("mult", rel - 2, "Q1"))
                for t in range(T1):
                    sp.dma_start(xd[:, s, t, :], rows(k, 4 * t, 1)).then_inc(x_loaded[s], 16)

            def load_xe(st, rel):
                if st.g + rel >= 1:
                    sp.wait_ge(mult, st.count("mult", rel - 1, "Q3"))
                for t in range(T1, TL):
                    sp.dma_start(xe[:, t - T1, :], rows(st.nth(rel - 1), 4 * t, 1)).then_inc(xe_loaded, 16)

            sp.wait_ge(w_turned, 6)
            for k in range(3):
                store_x(Step(k), 0)
                if k < 2:
                    load_x(Step(k), 0)
                if k == 1:
                    load_xe(Step(0), 0)

            def step(st):
                if st.g + 2 < G:
                    load_x(st, 2)
                if st.g + 1 < G:
                    load_xe(st, 1)
                if st.g + 3 < G:
                    store_x(st, 3)

            steps(sp, step)
            sp.wait_ge(y_ready, 1)
            sp.dma_start(out.rearrange("b a -> a b"), yrow).then_inc(y_out, 16)
            sp.wait_ge(y_out, 16)

        @block.gpsimd
        def _(pool):
            pool.wait_ge(ids_in, 16)
            for c in range(NC):
                for f in range(F):
                    pool.indirect_dma_start(
                        out=emb[:, f, c, :], out_offset=None, in_=tables[f],
                        in_offset=bass.IndirectOffsetOnAxis(ap=idx[:, c, f:f + 1], axis=0),
                    ).then_inc(gathered[c], 16)

            def low(st, rel, name):
                if mode(st.g + rel, name) != "P":
                    return
                s = slot(st.g + rel, name)
                pool.wait_ge(hi, st.count("hi", rel, name))
                pool.tensor_tensor(zl[:, s], zf[:, s], zh[:, s].bitcast(F32), ALU.subtract).then_inc(lo_p, 1)

            def step(st):
                if st.g < GA:
                    return
                for name in pairs(st.g):
                    low(st, 0, name)
                    if name == AFTER["add_dir2"] and st.g > GA:
                        add_dir2(pool, acc2_p, st, -1)
                    if name == AFTER["add_dir1"] and st.g % 2 == 0 and st.g < LAST:
                        add_dir1(pool, acc1_p, st)

            steps(pool, step)
            add_dir2(pool, acc2_p, Step(LAST), 0)

        @block.scalar
        def _(act):
            for b in range(5):
                act.wait_ge(w_turned, b + 1)
                dst = slice(4 * b, 4 * b + 4)
                for name in WHOLE:
                    t, _ = pair_tiles(name)
                    if t // 4 == b:
                        to = 2 * WHOLE.index(name)
                        act.activation(wf[:, to:to + 2].rearrange("p t n -> p (t n)"),
                                       banks[b][:, P * (t % 4):P * (t % 4) + 2 * P], ACT.Copy)
                act.activation(wh[:, dst].rearrange("p t n -> p (t n)"), banks[b], ACT.Copy).then_inc(w_high, 1)
            act.wait_ge(w_turned, 6)
            act.activation(wS[:], pt[:, 0, 0], ACT.Copy).then_inc(w_high, 1)
            act.activation(wSf[:], pt[:, 0, 0], ACT.Copy).then_inc(w_high, 1)
            act.wait_ge(consts_in, 64)
            act.wait_ge(zeroed, 1)

            def stage_x(st, rel):
                if st.g + rel >= 1:
                    act.wait_ge(turned, st.nth(rel - 1))
                cols = emb[:].rearrange("p f c d -> p f (c d)")[:, :, bass.ds(st.nth(rel - 1, ND), ND)].rearrange("p f d -> p d f")
                act.activation(stage[:, :, 2, :], cols, ACT.Copy).then_inc(stage_hi, 1)
                act.activation(stage[:, :, 0, :].bitcast(F32R), cols, ACT.Copy).then_inc(stage_hi, 1)

            def copy_xf(st, rel):
                act.wait_ge(turned, st.nth(rel))
                if st.g + rel >= 1:
                    act.wait_ge(x_stored, st.nth(rel - 1, 32))
                act.activation(xf[:], pt[2 * F:3 * F, (st.g + rel) % 2].rearrange("p a n -> p (a n)"), ACT.Copy).then_inc(xf_ready, 1)

            def copy_xs(st, rel):
                if st.g + rel >= 2:
                    act.wait_ge(fill, st.count("fill", rel - 2))
                act.activation(xs[0:2 * F, (st.g + rel) % 2], pt[0:2 * F, (st.g + rel) % 2].rearrange("p a n -> p (a n)"),
                               ACT.Copy).then_inc(xs_ready, 1)

            def high(st, name):
                if mode(st.g, name) == "F":
                    return
                s = slot(st.g, name)
                act.wait_ge(mult, st.count("mult", 0, name))
                prev = back(st.g, name, SLOTS)
                if prev is not None:
                    act.wait_ge(used, st.count("used", *prev))
                act.activation(zh[:, s], zf[:, s], ACT.Copy).then_inc(hi, 1)

            def high_s(st):
                act.wait_ge(s_mult, st.nth(1))
                if st.g >= 0:
                    act.wait_ge(y1_ready, st.nth(0))
                act.activation(zS[:], zSf[:], ACT.Copy).then_inc(s_hi, 1)

            def finish_1(st):
                s = (st.g + 1) % 2
                act.wait_ge(y1_ready, st.nth(1))
                if st.g >= 1:
                    act.wait_ge(mult, st.count("mult", -1, "Q7"))
                act.activation(hid[0:H, s], py1[0:H], ACT.Relu, bias=bias0[0:H]).then_inc(hid_ready, 1)
                act.activation(hid[H:P, s], py1[0:H], ACT.Relu, bias=bias0[0:H]).then_inc(hid_ready, 1)
                if s == 0 and st.g >= 1:
                    need_acc1(act, st, 0)
                act.activation(dir1[H * s:H * s + H], py1[H:P], ACT.Relu, bias=bias0[H:P]).then_inc(dir1_ready, 1)

            def finish_2(st, rel):
                act.wait_ge(used, st.count("used", rel, "Q7"))
                if st.g + rel >= 2:
                    need_acc2(act, st, rel - 2)
                act.activation(dir2[:, (st.g + rel) % 2], py2[:], ACT.Relu, bias=bias1[:]).then_inc(dir2_ready, 1)

            act.wait_ge(gathered[0], 16 * F)
            act.wait_ge(s_low, 3)
            for k in range(3):
                stage_x(Step(k), 0)
                if k < 2:
                    copy_xf(Step(k), 0)
                    copy_xs(Step(k), 0)
            start = Step(-1)
            for name in P_NAMES:
                high(start, name)
            high_s(start)
            copy_xf(Step(2), 0)
            finish_1(start)

            def step(st):
                if st.g == GA + 2:
                    for c in range(1, NC):
                        act.wait_ge(gathered[c], 16 * F)
                if st.g + 3 < G:
                    stage_x(st, 3)
                for name in pairs(st.g):
                    high(st, name)
                    if name == "P1":
                        high_s(st)
                    if name == AFTER["finish_2"] and st.g >= 1:
                        finish_2(st, -1)
                    if name == AFTER["finish_1"] and st.g < LAST:
                        finish_1(st)
                    if name == AFTER["copy_xf"] and st.g + 3 < G:
                        copy_xf(st, 3)
                    if name == AFTER["copy_xs"] and st.g + 2 < G:
                        copy_xs(st, 2)

            steps(act, step)
            finish_2(Step(LAST), 0)

            for m in range(4):
                act.wait_ge(top_mm, m + 1)
                act.activation(act1[:, m], top1[m], ACT.Relu, bias=bt1[:, m:m + 1]).then_inc(top_act, 1)
            for m in range(2):
                act.wait_ge(top_mm, 4 + m + 1)
                act.activation(act2[:, m], top2[m], ACT.Relu, bias=bt2[:, m:m + 1]).then_inc(top_act, 1)
            act.wait_ge(top_mm, 7)
            act.activation(yrow, px[0:1, 2], ACT.Copy).then_inc(y_ready, 1)

        @block.vector
        def _(dve):
            dve.memset(xs[2 * F:P].bitcast(F32), 0.0).then_inc(zeroed, 1)
            dve.memset(acc1[:], 0.0).then_inc(zeroed, 1)
            dve.wait_ge(cin_in, 48)
            dve.tensor_copy(w0_ext.rearrange("p (h a f) -> p h a f", a=2, f=F),
                            w0_twice[:, 0:1024].rearrange("p (h a f) -> p h a f", a=1, f=F)
                            .to_broadcast([P, F, 2, F])).then_inc(w_doubled, 1)
            dve.tensor_copy(w1_ext.rearrange("p (h a f) -> p h a f", a=2, f=F),
                            w1_nat.rearrange("p (h a f) -> p h a f", a=1, f=F)
                            .to_broadcast([P, H, 2, F])).then_inc(w_doubled, 1)
            dve.wait_ge(w_doubled, 2)
            straight = view(xd, 2048, [[1, 16], [2 * F + 1, F]])
            crossed = view(xd, 0, [[F, 16], [F + 1, F]])
            dve.tensor_tensor(sym.rearrange("p (r i) -> p r i", i=F), straight, crossed, ALU.add).then_inc(w_doubled, 1)
            dve.wait_ge(w_doubled, 3)
            dve.tensor_copy(sym[:, 0:F], view(xd, 2048, [[2 * F + 1, F]])).then_inc(w_doubled, 1)
            dve.tensor_copy(sym16.rearrange("p (j i) -> p j i", i=F),
                            view(xd, 2048 + 16, [[0, 4], [2 * F + 1, F]])).then_inc(w_doubled, 1)
            for odd in range(2):
                dve.tensor_copy(w1_rot[:, 1024 * odd:1024 * odd + 1024].rearrange("p (s u i) -> p s u i", u=2, i=F),
                                view(zf, odd, [[2, 16], [2 * F * F + 1, 2], [2 * F + 1, F]])).then_inc(w_doubled, 1)
            dve.wait_ge(consts_in, 64)
            dve.tensor_copy(spread[:].rearrange("p t (j i) -> p t j i", i=F),
                            view(bandf, 1, [[4, T2 - TL], [1, 4], [1, F]])).then_inc(w_doubled, 1)
            for b in range(5):
                dst = slice(4 * b, 4 * b + 4)
                dve.wait_ge(w_high, b + 1)
                dve.tensor_tensor(wl[:, dst].rearrange("p t n -> p (t n)"), banks[b],
                                  wh[:, dst].rearrange("p t n -> p (t n)").bitcast(F32), ALU.subtract).then_inc(w_low, 1)
            dve.wait_ge(w_high, 7)
            dve.tensor_tensor(wS[32:64], wSf[32:64], wS[32:64].bitcast(F32), ALU.subtract).then_inc(s_low, 1)
            dve.tensor_tensor(wS[96:128], wSf[96:128], wS[96:128].bitcast(F32), ALU.subtract).then_inc(s_low, 1)
            dve.wait_ge(top_in, 16 * 9)
            dve.wait_ge(s_low, 2)
            dve.wait_ge(dense_turned, 1)
            dve.tensor_copy(denseT[:], pt[0:16, 0].rearrange("p a n -> p (a n)")).then_inc(s_low, 1)

            def stage_low(st, rel):
                dve.wait_ge(stage_hi, st.nth(rel, 2))
                dve.tensor_tensor(stage[:, :, 1, :], stage[:, :, 2, :], stage[:, :, 0, :],
                                  ALU.subtract).then_inc(stage_lo, 1)

            def slot_free(st, name):
                prev = back(st.g, name, SLOTS)
                if prev is None:
                    return
                if mode(st.g + prev[0], prev[1]) == "F":
                    dve.wait_ge(used, st.count("used", *prev))
                else:
                    need_low(dve, st, *prev)

            def products(st, name):
                s = slot(st.g, name)
                _, t = pair_tiles(name)
                slot_free(st, name)
                if name[0] == "P":
                    x = (st.g + 1) % 2
                    if name == "P0":
                        dve.wait_ge(x_loaded[x], st.nth(1, 8 * (T1 + 2), 8 * (T1 + 2) * (1 - x)))
                    left, right = xd[:, x, t:t + 2, :], xd[:, x, T1:T1 + 1, :]
                else:
                    if name == "Q0":
                        dve.wait_ge(hid_ready, st.nth(0, 2))
                    if name in FILLED:
                        dve.wait_ge(fill, st.count("fill", 0, name))
                        left = px[:, t % 4:t % 4 + 2, :]
                    elif t >= T1:
                        if name == "Q2":
                            dve.wait_ge(xe_loaded, st.nth(0, 16 * (TL - T1)))
                        left = xe[:, t - T1:t - T1 + 2, :]
                    else:
                        left = xd[:, st.g % 2, t:t + 2, :]
                    right = hid[:, st.g % 2:st.g % 2 + 1, :]
                dve.tensor_tensor(zf[:, s], left, right.to_broadcast([P, 2, N]), ALU.mult).then_inc(mult, 1)

            def products_s(st):
                x = (st.g + 1) % 2
                need_s_low(dve, st, -1)
                dve.tensor_tensor(zSf[:], xd[:, x, T1 + 1, :], xd[:, x, T1, :], ALU.mult).then_inc(s_mult, 1)

            def low(st, rel, name):
                if mode(st.g + rel, name) != "V":
                    return
                s = slot(st.g + rel, name)
                dve.wait_ge(hi, st.count("hi", rel, name))
                dve.tensor_tensor(zl[:, s], zf[:, s], zh[:, s].bitcast(F32), ALU.subtract).then_inc(lo_v, 1)

            def low_s(st):
                if mode(st.g, "S") == "V":
                    dve.wait_ge(s_hi, st.nth(1))
                    dve.tensor_tensor(zS[H:P], zSf[H:P], zS[H:P].bitcast(F32), ALU.subtract).then_inc(slo_v, 1)

            def sum_d(a, acc, c0, c1):
                chunks_done = c1 * GC - GA
                dve.wait_ge((acc1_p, acc2_p)[a], chunks_done)
                dve.tensor_reduce(zsum[:, a, P * c0:P * c1].rearrange("p (c b) -> p c b", b=P),
                                  acc[:, c0:c1].rearrange("p c (d b) -> p c b d", d=ND),
                                  AX_X, ALU.add).then_inc(zsum_ready, 1)

            for k in range(3):
                stage_low(Step(k), 0)
            dve.wait_ge(w_turned, 6)
            dve.memset(acc2[:], 0.0).then_inc(zeroed, 1)
            dve.wait_ge(zeroed, 3)
            start = Step(-1)
            products(start, "P0")
            products(start, "P1")
            low(start, 0, "P0")
            products_s(start)
            low(start, 0, "P1")
            low_s(start)

            def step(st):
                for name in pairs(st.g):
                    products(st, name)
                    if name == "P1":
                        products_s(st)
                    behind = back(st.g, name, V_LAG)
                    if behind is not None and st.g + behind[0] >= 0:
                        low(st, *behind)
                    if name == "Q0" and st.g < LAST:
                        low_s(st)
                    if name == AFTER["stage_low"] and st.g + 3 < G:
                        stage_low(st, 3)
                    if name == AFTER["add_dir2"] and 1 <= st.g <= GA:
                        add_dir2(dve, acc2_v, st, -1)
                    if name == AFTER["add_dir1"] and st.g % 2 == 0 and st.g < GA:
                        add_dir1(dve, acc1_v, st)
                    if name == "Q5" and st.g == LAST - 2:
                        sum_d(0, acc1, 0, NC - 1)
                    if name == "Q5" and st.g == LAST - 1:
                        sum_d(1, acc2, 0, NC - 1)

            steps(dve, step)
            for name in pairs(LAST)[-V_LAG:]:
                low(Step(LAST), 0, name)

            sum_d(0, acc1, NC - 1, NC)
            sum_d(1, acc2, NC - 1, NC)

        @block.tensor
        def _(pe):
            pe.wait_ge(consts_in, 64)
            pe.wait_ge(w_doubled, 8)
            for t in range(T1 + T2):
                src = sym[:, P * t:P * t + P] if t < T1 else w1_rot[:, P * (t - T1):P * (t - T1) + P]
                tr = pe.transpose(banks[t // 4][:, P * (t % 4):P * (t % 4) + P], src, ident[:])
                if t % 4 == 3:
                    tr.then_inc(w_turned, 1)
            pe.transpose(pt[:, 0, 0], sym16, ident[:]).then_inc(w_turned, 1)
            pe.wait_ge(top_in, 16 * 9)
            pe.wait_ge(s_low, 2)
            for c in range(NC):
                tr = pe.transpose(pt[0:16, 0, c], dense[:, c, :], ident[:])
            tr.then_inc(dense_turned, 1)

            def turn_x(st, rel):
                pe.wait_ge(stage_lo, st.nth(rel))
                if st.g + rel >= 2:
                    pe.wait_ge(xs_ready, st.nth(rel - 2))
                for d in range(ND):
                    tr = pe.transpose(pt[0:3 * F, (st.g + rel) % 2, d], stage[:, d].rearrange("p a f -> p (a f)"), ident[:])
                tr.then_inc(turned, 1)

            def fill_x(st, name):
                _, t = pair_tiles(name)
                if name == FILLED[0]:
                    pe.wait_ge(xs_ready, st.nth(0))
                if name in FILLED[:2]:
                    if st.g >= 1:
                        pe.wait_ge(mult, st.count("mult", -1, FILLED[FILLED.index(name) - 2]))
                else:
                    pe.wait_ge(mult, st.count("mult", 0, FILLED[FILLED.index(name) - 2]))
                for h in range(2):
                    mm = pe.matmul(px[:, (t + h) % 4, :], spread[:, t + h - TL], xs[:, st.g % 2],
                                   start=True, stop=True)
                mm.then_inc(fill, 1)

            def layer(st, name):
                s = slot(st.g, name)
                w, _ = pair_tiles(name)
                bank = py1 if name[0] == "P" else py2
                first, last = name in ("P0", "Q0"), name == "Q7"
                if name == "P0" and st.g >= 0:
                    pe.wait_ge(dir1_ready, st.nth(0))
                if name == "Q0" and st.g >= 1:
                    pe.wait_ge(dir2_ready, st.nth(-1))
                if mode(st.g, name) == "F":
                    pe.wait_ge(mult, st.count("mult", 0, name))
                    for h in range(2):
                        mm = pe.matmul(bank[:], wf[:, 2 * WHOLE.index(name) + h], zf[:, s, h], start=first and h == 0, stop=last and h == 1)
                else:
                    pe.wait_ge(hi, st.count("hi", 0, name))
                    for h in range(2):
                        pe.matmul(bank[:], wh[:, w + h], zh[:, s, h], start=first and h == 0, stop=False)
                        pe.matmul(bank[:], wl[:, w + h], zh[:, s, h], start=False, stop=False)
                    need_low(pe, st, 0, name)
                    for h in range(2):
                        mm = pe.matmul(bank[:], wh[:, w + h], zl[:, s, h], start=False, stop=last and h == 1)
                mm.then_inc(used, 1)

            def layer_s(st):
                need_s_low(pe, st, 0)
                pe.matmul(py1[:], wS[:], zS[:], start=False, stop=True).then_inc(y1_ready, 1)

            pe.wait_ge(zeroed, 2)
            pe.wait_ge(s_low, 3)
            pe.wait_ge(w_low, 5)
            for k in range(3):
                turn_x(Step(k), 0)
            start = Step(-1)
            layer(start, "P0")
            layer(start, "P1")
            layer_s(start)

            def top_1(m, late):
                samples, cols = (slice(0, P * (NC - 1)), slice(P * (NC - 1), B))[late], slice(P * m, P * m + P)
                if m == 0:
                    pe.wait_ge(zsum_ready, 2 * late + 2)
                    pe.wait_ge(dir1_ready, G)
                pe.matmul(top1[m][:, samples], wt1c[:, cols], denseT[:, samples], start=True, stop=False)
                pe.matmul(top1[m][:, samples], wt1a[:, cols], zsum[:, 0, samples], start=False, stop=False)
                mm = pe.matmul(top1[m][:, samples], wt1b[:, cols], zsum[:, 1, samples], start=False, stop=True)
                if late:
                    mm.then_inc(top_mm, 1)

            def step(st):
                names = pairs(st.g)
                order = (P_NAMES + Q_NAMES)
                for name in order:
                    at = order.index(name) + LEAD
                    if name == "P0":
                        for early in order[:at + 1]:
                            if early in FILLED:
                                fill_x(st, early)
                    elif at < len(order) and order[at] in FILLED:
                        fill_x(st, order[at])
                    if name in names:
                        layer(st, name)
                    if name == "P1" and st.g < LAST:
                        layer_s(st)
                    if name == AFTER["turn_x"] and st.g + 3 < G:
                        turn_x(st, 3)
                    if st.g == LAST and name in TOP_AFTER:
                        top_1(TOP_AFTER.index(name), 0)

            steps(pe, step)

            top_1(3, 0)
            for m in range(4):
                top_1(m, 1)
            for m in range(2):
                for k in range(4):
                    if m == 0:
                        pe.wait_ge(top_act, k + 1)
                    mm = pe.matmul(top2[m], wt2[:, k, P * m:P * m + P], act1[:, k], start=k == 0, stop=k == 3)
                mm.then_inc(top_mm, 1)
            for k in range(2):
                pe.wait_ge(top_act, 4 + k + 1)
                mm = pe.matmul(px[0:1, 2], wt3[:, k:k + 1], act2[:, k], start=k == 0, stop=k == 1)
            mm.then_inc(top_mm, 1)


_SMALL = ["W_top1", "b_top1", "W_top2", "b_top2", "W_top3", "L0_rec_w0", "L0_rec_b0", "L0_rec_w1", "L0_rec_b1"]
_INS = ["dense_ctx", "ids"] + ["tbl_%d" % f for f in range(F)] + _SMALL


def kernel(**inputs):
    import concourse.bacc as _bacc
    from concourse.bass_utils import run_bass_kernel_spmd as _run

    nc = _bacc.Bacc("TRN2", target_bir_lowering=False, num_devices=1)
    arrays, args = {}, {}
    given = {name: np.ascontiguousarray(inputs[name]) for name in _INS}
    given["eye"] = np.eye(P, dtype=np.float32)
    row, col = np.arange(P)[:, None], np.arange(BAND)[None, :]
    given["band"] = ((row < 2 * F) & (row % F == col % F)).astype(np.float32)
    for name, a in given.items():
        arrays["in_" + name] = a
        args[name] = nc.dram_tensor("in_" + name, a.shape, mybir.dt.from_np(a.dtype), kind="ExternalInput").ap()
    out = nc.dram_tensor("out_0", (B, 1), F32, kind="ExternalOutput").ap()
    dlrm_tower(nc, args["dense_ctx"], args["ids"], [args["tbl_%d" % f] for f in range(F)],
               *[args[name] for name in _SMALL], args["eye"], args["band"], out)
    r = _run(nc, [arrays], core_ids=[0])
    return r.results[0]["out_0"]
```

```python
from contextlib import ExitStack

import concourse.bass as bass
from concourse import mybir
import numpy as np

F32 = mybir.dt.float32
F32R = mybir.dt.float32r
I32 = mybir.dt.int32
ALU = mybir.AluOpType
ACT = mybir.ActivationFunctionType
AX_X = mybir.AxisListType.X

P = 128
B, F, D = 512, 32, 64
H = 64
NC = B // P
ND = 4
N = ND * P
G = NC * D // ND
GC = D // ND
T1, T2 = 4, 16
TX = F // 4
SLOTS = 5
GA = 4

P_NAMES = ["P0", "P1"]
Q_NAMES = ["Q%d" % j for j in range(T2 // 2)]
ORDER = Q_NAMES[:2] + P_NAMES + Q_NAMES[2:]
LAST = G - 1

MODES = {
    "start": dict(P0="F", P1="V"),
    "gathering": dict(Q0="F", Q1="V", P0="F", P1="V", Q2="F", Q3="F", Q4="F", Q5="V", Q6="F", Q7="F"),
    "gathered": dict(Q0="F", Q1="V", P0="F", P1="V", Q2="F", Q3="F", Q4="F", Q5="V", Q6="F", Q7="F"),
    0: dict(Q0="F", Q1="P", P0="V", P1="P", Q2="P", Q3="F", Q4="P", Q5="F", Q6="P", Q7="V"),
    1: dict(Q0="F", Q1="P", P0="V", P1="P", Q2="P", Q3="F", Q4="P", Q5="F", Q6="P", Q7="F"),
    "last": dict(Q0="P", Q1="P", Q2="V", Q3="P", Q4="V", Q5="P", Q6="V", Q7="V"),
}
WHOLE = [n for n in P_NAMES + Q_NAMES if any(m.get(n) == "F" for m in MODES.values())]
V_LAG = 2
AFTER = dict(stage_x="Q0", turn_x="P0", copy_xf="Q2", finish_1="Q5", finish_swap="Q0", finish_2="Q2", add_dir1="Q5", add_dir2="Q3")
TOP_AFTER = ["Q2", "Q5"]


def mode(g, name):
    kind = ("start" if g < 0 else "gathering" if g < GA else "gathered" if g == GA else "last" if g == LAST
            else g % 2)
    return MODES[kind].get(name)


def pairs(g):
    if g < 0:
        return P_NAMES
    return ORDER if g < LAST else Q_NAMES


def events(kind, g):
    if kind == "mult":
        return pairs(g)
    if kind == "used_whole":
        return [n for n in pairs(g) if mode(g, n) == "F"]
    if kind in ("hi", "used_split"):
        return [n for n in pairs(g) if mode(g, n) != "F"]
    if kind in ("lo_v", "lo_p"):
        return [n for n in pairs(g) if mode(g, n) == kind[-1].upper()]
    raise ValueError(kind)


def back(g, name, by):
    at, rel = pairs(g).index(name) - by, 0
    while at < 0:
        rel -= 1
        if g + rel < -1:
            return None
        at += len(pairs(g + rel))
    return rel, pairs(g + rel)[at]


def closing(g):
    return "Q6" if mode(g, "Q7") == "F" and mode(g, "Q6") != "F" else "Q7"


def slot(g, name):
    return (sum(len(pairs(i)) for i in range(-1, g)) + pairs(g).index(name)) % SLOTS


class Step:

    def __init__(self, g, reg=None, reg0=0):
        self.g, self.reg, self.reg0 = g, reg, reg0

    def affine(self, value, per_turn):
        return value if self.reg is None else self.reg * per_turn + (value - per_turn * (self.reg0 // 2))

    def count(self, kind, rel=0, name=None):
        g = self.g + rel
        before = sum(len(events(kind, i)) for i in range(-1, g))
        own = events(kind, g)
        value = before + (len(own) if name is None else own.index(name) + 1)
        return self.affine(value, len(events(kind, self.g)) + len(events(kind, self.g + 1)))

    def nth(self, rel=0, per=1, off=0):
        return self.affine(per * (self.g + rel + 1) + off, 2 * per)


def need(eng, sem, value):
    if not isinstance(value, int) or value > 0:
        eng.wait_ge(sem, value)


def steps(eng, body):
    start, end = GA + 4, LAST - 3
    for g in range(start):
        body(Step(g))
    with eng.Fori(start // 2, end // 2) as turn:
        for u in range(2):
            body(Step(start + u, turn, start))
    for g in range(end, G):
        body(Step(g))


def view(t, offset, dims):
    whole = t[:]
    return bass.AP(tensor=whole.tensor, offset=offset, ap=[list(whole.ap[0])] + [list(d) for d in dims])


def dlrm_tower(nc, dense_ctx, ids, tables, W_top1, b_top1, W_top2, b_top2, W_top3, w0, b0, w1, b1,
               eye, out):
    with ExitStack() as ctx:
        def sb(name, shape, dt=F32):
            return ctx.enter_context(nc.sbuf_tensor(name, shape, dt))

        def sem(name):
            return ctx.enter_context(nc.semaphore(name))

        emb = sb("emb", [P, F, NC, D])
        idx = sb("idx", [P, NC, F], I32)
        wh = sb("wh", [P, T1 + T2, P], F32R)
        wl = sb("wl", [P, T1 + T2, P], F32R)
        wf = sb("wf", [P, 2 * len(WHOLE), P])
        wSf = sb("wSf", [P, P])
        wS = sb("wS", [P, P], F32R)
        ident = sb("ident", [P, P])
        bias0 = sb("bias0", [P, 1])
        bias1 = sb("bias1", [P, 1])
        xd = sb("xd", [P, 2, T1 + 2, N])
        xe = sb("xe", [P, TX - T1, N])
        stage = sb("stage", [P, ND, F])
        xf = sb("xf", [P, P])
        zf = sb("zf", [P, SLOTS, 2, N])
        zh = sb("zh", [P, SLOTS, 2, N], F32R)
        zl = sb("zl", [P, SLOTS, 2, N], F32R)
        zSf = sb("zSf", [P, N])
        zS = sb("zS", [P, N], F32R)
        hid = sb("hid", [P, 2, 2, N])
        dir1 = sb("dir1", [P, N])
        dir2 = sb("dir2", [P, 2, N])
        acc1 = sb("acc1", [P, NC, N])
        acc2 = sb("acc2", [P, NC, N])
        wt1a = sb("wt1a", [P, B])
        wt1b = sb("wt1b", [P, B])
        wt1c = sb("wt1c", [16, B])
        wt2 = sb("wt2", [P, 4, 256])
        wt3 = sb("wt3", [P, 2])
        bt1 = sb("bt1", [P, 4])
        bt2 = sb("bt2", [P, 2])
        dense = sb("dense", [P, NC, 16])
        denseT = sb("denseT", [16, B])

        xd_flat = xd[:].rearrange("p a t n -> p (a t n)")
        w0_twice = xd_flat[:, 0:2048]
        w0_ext = xd_flat[:, 2048:4096]
        w1_nat = xd_flat[:, 4096:6144]
        zf_flat = zf[:].rearrange("p a t n -> p (a t n)")
        w1_ext = zf_flat[:, 0:4096]
        sym = zf_flat[:, 4096:4096 + 512]
        sym16 = zf_flat[:, 4608:4608 + 128]
        acc2_flat = acc2[:].rearrange("p c n -> p (c n)")
        w1_rot = acc2_flat
        emb_flat = emb[:].rearrange("p f c d -> p (f c d)")
        zsum = emb_flat[:, 0:1024].rearrange("p (a n) -> p a n", a=2)
        act1 = emb_flat[:, 1024:3072].rearrange("p (m n) -> p m n", m=4)
        act2 = emb_flat[:, 3072:4096].rearrange("p (m n) -> p m n", m=2)
        yrow = emb_flat[0:1, 4096:4608]

        py1 = ctx.enter_context(nc.psum_tensor("py1", [P, 2, N], F32))
        py2 = ctx.enter_context(nc.psum_tensor("py2", [P, 2, N], F32))
        pt = ctx.enter_context(nc.psum_tensor("pt", [P, 2, N], F32))
        pm = ctx.enter_context(nc.psum_tensor("pm", [P, 2, N], F32))
        banks = [py1[:, 0], py1[:, 1], py2[:, 0], py2[:, 1], pm[:, 0]]
        top1 = [pm[:, 0], pm[:, 1], pt[:, 0], pt[:, 1]]
        top2 = [py1[:, 0], py1[:, 1]]

        x_dram = nc.dram_tensor("x_dram", [G, 2 * F, N], F32, kind="Internal")

        ids_in = sem("ids_in")
        consts_in = sem("consts_in")
        cin_in = sem("cin_in")
        top_in = sem("top_in")
        gathered = [sem("gathered%d" % c) for c in range(NC)]
        zeroed = sem("zeroed")
        w_doubled = sem("w_doubled")
        w_turned = sem("w_turned")
        w_high = sem("w_high")
        w_low = sem("w_low")
        s_low = sem("s_low")
        staged = sem("staged")
        turned = sem("turned")
        xf_ready = sem("xf_ready")
        x_stored = sem("x_stored")
        x_loaded = [sem("x_loaded0"), sem("x_loaded1")]
        x_first = sem("x_first")
        xe_loaded = sem("xe_loaded")
        mult = sem("mult")
        hi = sem("hi")
        lo_v = sem("lo_v")
        lo_p = sem("lo_p")
        used_whole = sem("used_whole")
        used_split = sem("used_split")
        s_mult = sem("s_mult")
        s_hi = sem("s_hi")
        s_lo = sem("s_lo")
        y1_ready = sem("y1_ready")
        hid_ready = sem("hid_ready")
        dir1_ready = sem("dir1_ready")
        dir2_ready = sem("dir2_ready")
        acc1_v, acc1_p = sem("acc1_v"), sem("acc1_p")
        acc2_v, acc2_p = sem("acc2_v"), sem("acc2_p")
        zsum_ready = sem("zsum_ready")
        dense_turned = sem("dense_turned")
        top_mm, top_act = sem("top_mm"), sem("top_act")
        y_ready, y_out = sem("y_ready"), sem("y_out")

        lo_sem = {"V": lo_v, "P": lo_p}
        lo_kind = {"V": "lo_v", "P": "lo_p"}

        def need_low(eng, st, rel, name):
            m = mode(st.g + rel, name)
            need(eng, lo_sem[m], st.count(lo_kind[m], rel, name))

        def need_used(eng, st, rel, name):
            if mode(st.g + rel, name) == "F":
                need(eng, used_whole, st.count("used_whole", rel, name))
            else:
                need(eng, used_split, st.count("used_split", rel, name))

        def need_s_low(eng, st, rel):
            need(eng, s_lo, st.nth(rel + 1))

        def weight_tile(name):
            return 2 * int(name[1]) + (0 if name[0] == "P" else T1)

        def need_acc1(eng, st, rel):
            if st.g + rel < GA:
                need(eng, acc1_v, st.nth(rel))
            else:
                need(eng, acc1_p, st.nth(rel, off=-GA))

        def need_acc2(eng, st, rel):
            if st.g + rel < GA:
                need(eng, acc2_v, st.nth(rel))
            else:
                need(eng, acc2_p, st.nth(rel, off=-GA))

        def chunk_sum(acc, st, rel):
            if st.reg is None:
                return acc[:, (st.g + rel) // GC, :]
            return acc[:, bass.ds(st.nth(rel - 1) // GC, 1), :].rearrange("p a n -> p (a n)")

        def add_dir2(eng, done, st, rel):
            eng.wait_ge(dir2_ready, st.nth(rel))
            s = chunk_sum(acc2, st, rel)
            if st.g + rel > 0:
                need_acc2(eng, st, rel - 1)
            eng.tensor_tensor(s, s, dir2[:, (st.g + rel) % 2, :], ALU.add).then_inc(done, 1)

        def add_dir1(eng, done, st):
            eng.wait_ge(dir1_ready, st.nth(0))
            s = chunk_sum(acc1, st, 0)
            if st.g > 1:
                need_acc1(eng, st, -2)
            eng.tensor_tensor(s, s, dir1[:], ALU.add).then_inc(done, 2)

        block = ctx.enter_context(nc.Block())

        @block.sync
        def _(sp):
            sp.dma_start(idx[:], ids.rearrange("(c p) f -> p c f", p=P)).then_inc(ids_in, 16)
            sp.dma_start(ident[:], eye).then_inc(consts_in, 16)
            sp.dma_start(w0_twice[:, 0:1024], w0).then_inc(cin_in, 16)
            sp.dma_start(w0_twice[:, 1024:2048], w0).then_inc(cin_in, 16)
            sp.dma_start(w1_nat, w1).then_inc(cin_in, 16)
            sp.dma_start(bias0[:], b0.rearrange("(p a) -> p a", a=1)).then_inc(consts_in, 16)
            sp.dma_start(bias1[:], b1.rearrange("(p a) -> p a", a=1)).then_inc(consts_in, 16)
            for half in range(2):
                sp.dma_start(wt1a[H * half:H * half + H, :], W_top1[0:H, :]).then_inc(top_in, 16)
            sp.dma_start(wt1b[:], W_top1[H:H + P, :]).then_inc(top_in, 16)
            sp.dma_start(wt1c[:], W_top1[H + P:H + P + 16, :]).then_inc(top_in, 16)
            sp.dma_start(wt2[:], W_top2.rearrange("(k p) n -> p k n", p=P)).then_inc(top_in, 16)
            sp.dma_start(wt3[:], W_top3.rearrange("(k p) n -> p (k n)", p=P), allow_slow_non_contiguous=True).then_inc(top_in, 16)
            sp.dma_start(bt1[:], b_top1.rearrange("(k p) -> p k", p=P), allow_slow_non_contiguous=True).then_inc(top_in, 16)
            sp.dma_start(bt2[:], b_top2.rearrange("(k p) -> p k", p=P), allow_slow_non_contiguous=True).then_inc(top_in, 16)
            sp.dma_start(dense[:], dense_ctx.rearrange("(c p) n -> p c n", p=P)).then_inc(top_in, 16)

            def store_x(st, rel):
                sp.wait_ge(xf_ready, st.nth(rel))
                for half in range(2):
                    dst = x_dram[bass.ds(st.nth(rel - 1), 1), F * half:F * half + 1, :]
                    sp.dma_start(bass.AP(tensor=dst.tensor, offset=dst.offset, ap=[[P, ND], [N, F], [1, P]]),
                                 xf[:]).then_inc(x_stored, 16)

            def rows(k, r, dj):
                src = x_dram[bass.ds(k, 1), r:r + 1, :]
                return bass.AP(tensor=src.tensor, offset=src.offset, ap=[[dj * N, 4], [N, F], [1, N]])

            def load_x(st, rel):
                s, k = (st.g + rel) % 2, st.nth(rel - 1)
                sp.wait_ge(x_stored, st.nth(rel, 32))
                if st.g + rel >= 2:
                    sp.wait_ge(s_mult, st.nth(rel - 2))
                early = x_first if st.g + rel == 0 else x_loaded[s]
                sp.dma_start(xd[:, s, T1, :], rows(k, 0, 0)).then_inc(early, 16)
                if st.g + rel == 0:
                    for t in range(2):
                        sp.dma_start(xd[:, s, t, :], rows(k, 4 * t, 1)).then_inc(early, 16)
                sp.dma_start(xd[:, s, T1 + 1, :], rows(k, 16, 0)).then_inc(x_loaded[s], 16)
                if st.g + rel >= 2:
                    sp.wait_ge(mult, st.count("mult", rel - 2, "Q3"))
                for t in range(2 if st.g + rel == 0 else 0, T1):
                    sp.dma_start(xd[:, s, t, :], rows(k, 4 * t, 1)).then_inc(x_loaded[s], 16)

            def load_xe(st, rel):
                if st.g + rel >= 1:
                    sp.wait_ge(mult, st.count("mult", rel - 1, "Q7"))
                for t in range(T1, TX):
                    sp.dma_start(xe[:, t - T1, :], rows(st.nth(rel - 1), 4 * t, 1)).then_inc(xe_loaded, 16)

            sp.wait_ge(w_turned, 6)
            for k in range(3):
                store_x(Step(k), 0)
                if k < 2:
                    load_x(Step(k), 0)
                if k == 1:
                    load_xe(Step(0), 0)

            def step(st):
                if st.g + 2 < G:
                    load_x(st, 2)
                if st.g + 3 < G:
                    store_x(st, 3)
                if st.g + 1 < G:
                    load_xe(st, 1)

            steps(sp, step)
            sp.wait_ge(y_ready, 1)
            sp.dma_start(out.rearrange("b a -> a b"), yrow).then_inc(y_out, 16)
            sp.wait_ge(y_out, 16)

        @block.gpsimd
        def _(pool):
            pool.wait_ge(ids_in, 16)
            for c in range(NC):
                for f in range(F):
                    pool.indirect_dma_start(
                        out=emb[:, f, c, :], out_offset=None, in_=tables[f],
                        in_offset=bass.IndirectOffsetOnAxis(ap=idx[:, c, f:f + 1], axis=0),
                    ).then_inc(gathered[c], 16)

            def low(st, rel, name):
                if mode(st.g + rel, name) != "P":
                    return
                s = slot(st.g + rel, name)
                pool.wait_ge(hi, st.count("hi", rel, name))
                pool.tensor_tensor(zl[:, s], zf[:, s], zh[:, s].bitcast(F32), ALU.subtract).then_inc(lo_p, 1)

            def step(st):
                if st.g < GA:
                    return
                for name in pairs(st.g):
                    low(st, 0, name)
                    if name == AFTER["add_dir2"] and st.g > GA:
                        add_dir2(pool, acc2_p, st, -1)
                    if name == AFTER["add_dir1"] and st.g % 2 == 1:
                        add_dir1(pool, acc1_p, st)

            steps(pool, step)
            add_dir2(pool, acc2_p, Step(LAST), 0)

        @block.scalar
        def _(act):
            for b in range(5):
                act.wait_ge(w_turned, b + 1)
                dst = slice(4 * b, 4 * b + 4)
                for name in WHOLE:
                    t = weight_tile(name)
                    if t // 4 == b:
                        to = 2 * WHOLE.index(name)
                        act.activation(wf[:, to:to + 2].rearrange("p t n -> p (t n)"),
                                       banks[b][:, P * (t % 4):P * (t % 4) + 2 * P], ACT.Copy)
                act.activation(wh[:, dst].rearrange("p t n -> p (t n)"), banks[b], ACT.Copy).then_inc(w_high, 1)
            act.wait_ge(w_turned, 6)
            act.activation(wS[:], pt[:, 0, 0:P], ACT.Copy).then_inc(w_high, 1)
            act.activation(wSf[:], pt[:, 0, 0:P], ACT.Copy).then_inc(w_high, 1)
            act.wait_ge(consts_in, 48)

            def stage_x(st, rel):
                if st.g + rel >= 1:
                    act.wait_ge(turned, st.nth(rel - 1))
                cols = emb[:].rearrange("p f c d -> p f (c d)")[:, :, bass.ds(st.nth(rel - 1, ND), ND)].rearrange("p f d -> p d f")
                act.activation(stage[:], cols, ACT.Copy).then_inc(staged, 1)

            def copy_xf(st, rel):
                act.wait_ge(turned, st.nth(rel))
                if st.g + rel >= 1:
                    act.wait_ge(x_stored, st.nth(rel - 1, 32))
                act.activation(xf[:], pt[:, (st.g + rel) % 2, 0:P], ACT.Copy).then_inc(xf_ready, 1)

            def high(st, name):
                if mode(st.g, name) == "F":
                    return
                s = slot(st.g, name)
                act.wait_ge(mult, st.count("mult", 0, name))
                prev = back(st.g, name, SLOTS)
                if prev is not None:
                    need_used(act, st, *prev)
                act.activation(zh[:, s], zf[:, s], ACT.Copy).then_inc(hi, 1)

            def high_s(st):
                act.wait_ge(s_mult, st.nth(1))
                if st.g >= 0:
                    act.wait_ge(y1_ready, st.nth(0))
                act.activation(zS[:], zSf[:], ACT.Copy).then_inc(s_hi, 1)

            def finish_1(st):
                s = (st.g + 1) % 2
                act.wait_ge(y1_ready, st.nth(1))
                if st.g >= 1:
                    act.wait_ge(mult, st.count("mult", -1, "Q7"))
                y = py1[:, s]
                act.activation(hid[0:H, s, 0], y[0:H], ACT.Relu, bias=bias0[0:H]).then_inc(hid_ready, 1)
                act.activation(hid[H:P, s, 0], y[0:H], ACT.Relu, bias=bias0[0:H]).then_inc(hid_ready, 1)

            def finish_swap(st):
                s = st.g % 2
                y = py1[:, s]
                act.activation(hid[0:F, s, 1], y[F:H], ACT.Relu, bias=bias0[F:H]).then_inc(hid_ready, 1)
                act.activation(hid[F:H, s, 1], y[0:F], ACT.Relu, bias=bias0[0:F]).then_inc(hid_ready, 1)
                act.wait_ge(hid_ready, st.nth(0, 5, -1))
                act.activation(hid[H:P, s, 1], hid[0:H, s, 1], ACT.Copy).then_inc(hid_ready, 1)
                if s == 0 and st.g >= 1:
                    need_acc1(act, st, -1)
                act.activation(dir1[H * s:H * s + H], y[H:P], ACT.Relu, bias=bias0[H:P]).then_inc(dir1_ready, 1)

            def finish_2(st, rel):
                need_used(act, st, rel, closing(st.g + rel))
                if st.g + rel >= 2:
                    need_acc2(act, st, rel - 2)
                act.activation(dir2[:, (st.g + rel) % 2], py2[:, (st.g + rel) % 2], ACT.Relu, bias=bias1[:]).then_inc(dir2_ready, 1)

            act.wait_ge(gathered[0], 16 * F)
            for k in range(3):
                stage_x(Step(k), 0)
                if k < 2:
                    copy_xf(Step(k), 0)
            start = Step(-1)
            for name in P_NAMES:
                high(start, name)
            high_s(start)
            copy_xf(Step(2), 0)
            finish_1(start)

            def step(st):
                if st.g == GA + 2:
                    for c in range(1, NC):
                        act.wait_ge(gathered[c], 16 * F)
                for name in pairs(st.g):
                    high(st, name)
                    if name == AFTER["stage_x"] and st.g + 3 < G:
                        stage_x(st, 3)
                    if name == "P1":
                        high_s(st)
                    if name == AFTER["finish_2"] and st.g >= 1:
                        finish_2(st, -1)
                    if name == AFTER["finish_swap"]:
                        finish_swap(st)
                    if name == AFTER["finish_1"] and st.g < LAST:
                        finish_1(st)
                    if name == AFTER["copy_xf"] and st.g + 3 < G:
                        copy_xf(st, 3)

            steps(act, step)
            finish_2(Step(LAST), 0)

            for m in range(4):
                act.wait_ge(top_mm, m + 1)
                act.activation(act1[:, m], top1[m], ACT.Relu, bias=bt1[:, m:m + 1]).then_inc(top_act, 1)
            for m in range(2):
                act.wait_ge(top_mm, 4 + m + 1)
                act.activation(act2[:, m], top2[m], ACT.Relu, bias=bt2[:, m:m + 1]).then_inc(top_act, 1)
            act.wait_ge(top_mm, 7)
            act.activation(yrow, py2[0:1, 0], ACT.Copy).then_inc(y_ready, 1)

        @block.vector
        def _(dve):
            dve.memset(acc1[:], 0.0).then_inc(zeroed, 1)
            dve.wait_ge(cin_in, 48)
            dve.tensor_copy(w0_ext.rearrange("p (h a f) -> p h a f", a=2, f=F),
                            w0_twice[:, 0:1024].rearrange("p (h a f) -> p h a f", a=1, f=F)
                            .to_broadcast([P, F, 2, F])).then_inc(w_doubled, 1)
            dve.tensor_copy(w1_ext.rearrange("p (h a f) -> p h a f", a=2, f=F),
                            w1_nat.rearrange("p (h a f) -> p h a f", a=1, f=F)
                            .to_broadcast([P, H, 2, F])).then_inc(w_doubled, 1)
            dve.wait_ge(w_doubled, 2)
            straight = view(xd, 2048, [[1, 16], [2 * F + 1, F]])
            crossed = view(xd, 0, [[F, 16], [F + 1, F]])
            dve.tensor_tensor(sym.rearrange("p (r i) -> p r i", i=F), straight, crossed, ALU.add).then_inc(w_doubled, 1)
            dve.wait_ge(w_doubled, 3)
            dve.tensor_copy(sym[:, 0:F], view(xd, 2048, [[2 * F + 1, F]])).then_inc(w_doubled, 1)
            dve.tensor_copy(sym16.rearrange("p (j i) -> p j i", i=F),
                            view(xd, 2048 + 16, [[0, 4], [2 * F + 1, F]])).then_inc(w_doubled, 1)
            for half in range(2):
                for swap in range(2):
                    for u in range(2):
                        group = w1_rot[:, 512 * (2 * half + swap):512 * (2 * half + swap) + 512]
                        dve.tensor_copy(group.rearrange("p (s u i) -> p s u i", u=2, i=F)[:, :, u],
                                        view(zf, F * (u ^ swap) * 2 * F + 16 * half + u, [[2, 8], [2 * F + 1, F]])
                                        ).then_inc(w_doubled, 1)
            for b in range(5):
                dst = slice(4 * b, 4 * b + 4)
                dve.wait_ge(w_high, b + 1)
                dve.tensor_tensor(wl[:, dst].rearrange("p t n -> p (t n)"), banks[b],
                                  wh[:, dst].rearrange("p t n -> p (t n)").bitcast(F32), ALU.subtract).then_inc(w_low, 1)
            dve.wait_ge(w_high, 7)
            dve.tensor_tensor(wS[32:64], wSf[32:64], wS[32:64].bitcast(F32), ALU.subtract).then_inc(s_low, 1)
            dve.tensor_tensor(wS[96:128], wSf[96:128], wS[96:128].bitcast(F32), ALU.subtract).then_inc(s_low, 1)
            dve.wait_ge(top_in, 16 * 9)
            dve.wait_ge(s_low, 2)
            dve.wait_ge(dense_turned, 1)
            dve.tensor_copy(denseT[:], pm[0:16, 1]).then_inc(s_low, 1)

            def slot_free(st, name):
                prev = back(st.g, name, SLOTS)
                if prev is None:
                    return
                if mode(st.g + prev[0], prev[1]) == "F":
                    need_used(dve, st, *prev)
                else:
                    need_low(dve, st, *prev)

            def products(st, name):
                s = slot(st.g, name)
                slot_free(st, name)
                if name[0] == "P":
                    x, t = (st.g + 1) % 2, weight_tile(name)
                    if name == "P0" and st.g < 0:
                        dve.wait_ge(x_first, 16 * 3)
                    if name == ("P0" if st.g >= 0 else "P1"):
                        dve.wait_ge(x_loaded[x], st.nth(1, 8 * (T1 + 2), (8 * (T1 + 2) - 16 * 3) * (1 - x)))
                    left, right = xd[:, x, t:t + 2, :], xd[:, x, T1:T1 + 1, :]
                else:
                    k = int(name[1])
                    t, swap = 2 * (k % 2), k // 2 % 2
                    if name == "Q0":
                        dve.wait_ge(hid_ready, st.nth(0, 5, -3))
                    if name == "Q2":
                        dve.wait_ge(hid_ready, st.nth(0, 5))
                    if name == "Q4":
                        dve.wait_ge(xe_loaded, st.nth(0, 16 * (TX - T1)))
                    left = xe[:, t:t + 2, :] if k >= 4 else xd[:, st.g % 2, t:t + 2, :]
                    right = hid[:, st.g % 2, swap:swap + 1, :]
                dve.tensor_tensor(zf[:, s], left, right.to_broadcast([P, 2, N]), ALU.mult).then_inc(mult, 1)

            def products_s(st):
                x = (st.g + 1) % 2
                need_s_low(dve, st, -1)
                dve.tensor_tensor(zSf[:], xd[:, x, T1 + 1, :], xd[:, x, T1, :], ALU.mult).then_inc(s_mult, 1)

            def low(st, rel, name):
                if mode(st.g + rel, name) != "V":
                    return
                s = slot(st.g + rel, name)
                dve.wait_ge(hi, st.count("hi", rel, name))
                dve.tensor_tensor(zl[:, s], zf[:, s], zh[:, s].bitcast(F32), ALU.subtract).then_inc(lo_v, 1)

            def low_s(st):
                dve.wait_ge(s_hi, st.nth(1))
                dve.tensor_tensor(zS[H:P], zSf[H:P], zS[H:P].bitcast(F32), ALU.subtract).then_inc(s_lo, 1)

            def sum_d(a, acc, c0, c1):
                chunks_done = c1 * GC - GA
                dve.wait_ge((acc1_p, acc2_p)[a], chunks_done)
                dve.tensor_reduce(zsum[:, a, P * c0:P * c1].rearrange("p (c b) -> p c b", b=P),
                                  acc[:, c0:c1].rearrange("p c (d b) -> p c b d", d=ND),
                                  AX_X, ALU.add).then_inc(zsum_ready, 1)

            dve.wait_ge(w_turned, 6)
            dve.memset(acc2[:], 0.0).then_inc(zeroed, 1)
            dve.wait_ge(zeroed, 2)
            start = Step(-1)
            products(start, "P0")
            products(start, "P1")
            low(start, 0, "P0")
            products_s(start)
            low(start, 0, "P1")
            low_s(start)

            def step(st):
                for name in pairs(st.g):
                    products(st, name)
                    if name == "P1":
                        products_s(st)
                    behind = back(st.g, name, V_LAG)
                    if behind is not None and st.g + behind[0] >= 0:
                        low(st, *behind)
                    if name == "Q2" and st.g < LAST:
                        low_s(st)
                    if name == AFTER["add_dir2"] and 1 <= st.g <= GA:
                        add_dir2(dve, acc2_v, st, -1)
                    if name == AFTER["add_dir1"] and st.g % 2 == 1 and st.g < GA:
                        add_dir1(dve, acc1_v, st)
                    if name == "Q5" and st.g == LAST - 2:
                        dve.wait_ge(turned, G)
                        sum_d(0, acc1, 0, NC - 1)
                    if name == "Q5" and st.g == LAST - 1:
                        sum_d(1, acc2, 0, NC - 1)

            steps(dve, step)
            for name in pairs(LAST)[-V_LAG:]:
                low(Step(LAST), 0, name)

            sum_d(0, acc1, NC - 1, NC)
            sum_d(1, acc2, NC - 1, NC)

        @block.tensor
        def _(pe):
            pe.wait_ge(consts_in, 48)
            pe.wait_ge(w_doubled, 5 + 8)
            for t in range(T1 + T2):
                src = sym[:, P * t:P * t + P] if t < T1 else w1_rot[:, P * (t - T1):P * (t - T1) + P]
                tr = pe.transpose(banks[t // 4][:, P * (t % 4):P * (t % 4) + P], src, ident[:])
                if t % 4 == 3:
                    tr.then_inc(w_turned, 1)
            pe.transpose(pt[:, 0, 0:P], sym16, ident[:]).then_inc(w_turned, 1)
            pe.wait_ge(top_in, 16 * 9)
            for c in range(NC):
                tr = pe.transpose(pm[0:16, 1, P * c:P * c + P], dense[:, c, :], ident[:])
            tr.then_inc(dense_turned, 1)

            def turn_x(st, rel):
                pe.wait_ge(staged, st.nth(rel))
                if st.g + rel >= 2:
                    pe.wait_ge(xf_ready, st.nth(rel - 2))
                pe.transpose(pt[:, (st.g + rel) % 2, 0:P], stage[:].rearrange("p d f -> p (d f)"),
                             ident[:]).then_inc(turned, 1)

            def bank(st, name):
                return py1[:, (st.g + 1) % 2] if name[0] == "P" else py2[:, st.g % 2]

            def layer(st, name):
                s, w, y = slot(st.g, name), weight_tile(name), bank(st, name)
                first = name in ("P0", "Q0")
                if name == "P0" and st.g >= 1:
                    pe.wait_ge(dir1_ready, st.nth(-1))
                if name == "Q0" and st.g >= 2:
                    pe.wait_ge(dir2_ready, st.nth(-2))
                if mode(st.g, name) == "F":
                    last = closing(st.g) == name
                    pe.wait_ge(mult, st.count("mult", 0, name))
                    for h in range(2):
                        mm = pe.matmul(y, wf[:, 2 * WHOLE.index(name) + h], zf[:, s, h], start=first and h == 0, stop=last and h == 1)
                    mm.then_inc(used_whole, 1)
                else:
                    pe.wait_ge(hi, st.count("hi", 0, name))
                    for h in range(2):
                        pe.matmul(y, wh[:, w + h], zh[:, s, h], start=first and h == 0, stop=False)
                        pe.matmul(y, wl[:, w + h], zh[:, s, h], start=False, stop=False)

            def layer_low(st, rel, name):
                if mode(st.g + rel, name) == "F":
                    return
                at = Step(st.g + rel)
                s, w, y, last = slot(at.g, name), weight_tile(name), bank(at, name), closing(at.g) == name
                need_low(pe, st, rel, name)
                for h in range(2):
                    mm = pe.matmul(y, wh[:, w + h], zl[:, s, h], start=False, stop=last and h == 1)
                mm.then_inc(used_split, 1)

            def layer_s(st):
                need_s_low(pe, st, 0)
                pe.matmul(py1[:, (st.g + 1) % 2], wS[:], zS[:], start=False, stop=True).then_inc(y1_ready, 1)

            pe.wait_ge(s_low, 2)
            pe.wait_ge(w_low, 5)
            for k in range(3):
                turn_x(Step(k), 0)
            start = Step(-1)
            for name in P_NAMES:
                layer(start, name)
                layer_low(start, 0, name)
            layer_s(start)

            def top_1(m, late):
                samples, cols = (slice(0, P * (NC - 1)), slice(P * (NC - 1), B))[late], slice(P * m, P * m + P)
                if m == 0:
                    pe.wait_ge(zsum_ready, 2 * late + 2)
                    pe.wait_ge(xf_ready, G)
                pe.matmul(top1[m][:, samples], wt1c[:, cols], denseT[:, samples], start=True, stop=False)
                pe.matmul(top1[m][:, samples], wt1a[:, cols], zsum[:, 0, samples], start=False, stop=False)
                mm = pe.matmul(top1[m][:, samples], wt1b[:, cols], zsum[:, 1, samples], start=False, stop=True)
                if late:
                    mm.then_inc(top_mm, 1)

            def step(st):
                for name in pairs(st.g):
                    layer(st, name)
                    behind = back(st.g, name, 1)
                    if st.g + behind[0] >= 0:
                        layer_low(st, *behind)
                    if name == "Q2" and st.g < LAST:
                        layer_s(st)
                    if name == AFTER["turn_x"] and st.g + 3 < G:
                        turn_x(st, 3)
                    if st.g == LAST and name in TOP_AFTER:
                        top_1(TOP_AFTER.index(name), 0)

            steps(pe, step)

            layer_low(Step(LAST), 0, "Q7")

            for m in range(len(TOP_AFTER), 4):
                top_1(m, 0)
            for m in range(4):
                top_1(m, 1)
            for m in range(2):
                for k in range(4):
                    if m == 0:
                        pe.wait_ge(top_act, k + 1)
                    mm = pe.matmul(top2[m], wt2[:, k, P * m:P * m + P], act1[:, k], start=k == 0, stop=k == 3)
                mm.then_inc(top_mm, 1)
            for k in range(2):
                pe.wait_ge(top_act, 4 + k + 1)
                mm = pe.matmul(py2[0:1, 0], wt3[:, k:k + 1], act2[:, k], start=k == 0, stop=k == 1)
            mm.then_inc(top_mm, 1)


_SMALL = ["W_top1", "b_top1", "W_top2", "b_top2", "W_top3", "L0_rec_w0", "L0_rec_b0", "L0_rec_w1", "L0_rec_b1"]
_INS = ["dense_ctx", "ids"] + ["tbl_%d" % f for f in range(F)] + _SMALL


def kernel(**inputs):
    import concourse.bacc as _bacc
    from concourse.bass_utils import run_bass_kernel_spmd as _run

    nc = _bacc.Bacc("TRN2", target_bir_lowering=False, num_devices=1)
    arrays, args = {}, {}
    given = {name: np.ascontiguousarray(inputs[name]) for name in _INS}
    given["eye"] = np.eye(P, dtype=np.float32)
    for name, a in given.items():
        arrays["in_" + name] = a
        args[name] = nc.dram_tensor("in_" + name, a.shape, mybir.dt.from_np(a.dtype), kind="ExternalInput").ap()
    out = nc.dram_tensor("out_0", (B, 1), F32, kind="ExternalOutput").ap()
    dlrm_tower(nc, args["dense_ctx"], args["ids"], [args["tbl_%d" % f] for f in range(F)],
               *[args[name] for name in _SMALL], args["eye"], out)
    r = _run(nc, [arrays], core_ids=[0])
    return r.results[0]["out_0"]
```
